# Optimizing a Trainium2 kernel written in Bass

```python
import numpy as np
import jax
import jax.numpy as jnp

def _softmax(x, axis=-1):
    return jax.nn.softmax(x, axis=axis)

def _gelu(x):
    return jax.nn.gelu(x, approximate=True)

def _silu(x):
    return jax.nn.silu(x)

def _sigmoid(x):
    return jax.nn.sigmoid(x)

def _layernorm(x, axis=-1, eps=1e-05):
    m = jnp.mean(x, axis=axis, keepdims=True)
    v = jnp.var(x, axis=axis, keepdims=True)
    return (x - m) / jnp.sqrt(v + eps)

def _scatter_add(tgt, idx, src, axis=0):
    return tgt.at[idx].add(src)

def _segment_sum(src, seg, n):
    return jax.ops.segment_sum(src, seg, n)
kernel_name = 'mk_xattn_ffn_d1_seqx_r8_f58787'

def setup_inputs(seed: int=0):
    np.random.seed(seed)
    _w = jnp.asarray

    def _rec_inputs():
        import jax
        import jax.numpy as jnp
        _rk = jax.random.key(seed)
        x = -0.0002928 + 1 * jax.random.normal(jax.random.fold_in(_rk, 1), (64, 64, 128), jnp.float32)
        _lenS = 64 - jax.random.randint(jax.random.fold_in(_rk, 7), (64,), 0, max(1, 64 // 4) + 1, jnp.int32)
        _lenS2 = 64 - jax.random.randint(jax.random.fold_in(_rk, 8), (64,), 0, max(1, 64 // 4) + 1, jnp.int32)
        _ctx_1024P = jax.random.normal(jax.random.fold_in(_rk, 11), (64, 16, 128), jnp.float32)
        _ctx_1024c = jax.random.dirichlet(jax.random.fold_in(_rk, 511), 0.3 * jnp.ones((16,), jnp.float32), (64, 64))
        _ctx_1024t = jnp.einsum('bsk,bkd->bsd', _ctx_1024c, _ctx_1024P)
        _ctx_1024t = _ctx_1024t * jax.lax.rsqrt(jnp.mean(jnp.square(_ctx_1024t)) + 1e-12) * 0.953939
        ctx_1024 = -1.39393e-06 + 0.999914 * (_ctx_1024t + 0.3 * jax.random.normal(jax.random.fold_in(_rk, 611), (64, 64, 128), jnp.float32))
        _validS = jnp.arange(64)[None, :] < _lenS[:, None]
        _validS2 = jnp.arange(64)[None, :] < _lenS2[:, None]
        _causal = jnp.tril(jnp.ones((64, 64), dtype=bool))
        mask_Bx16xSxS2_ff0 = jnp.where(jnp.ones((64, 16, 64, 64), dtype=bool), 0.0, -1000000000.0).astype(jnp.float32)
        return (x, ctx_1024, mask_Bx16xSxS2_ff0)
    x, ctx_1024, mask_Bx16xSxS2_ff0 = _rec_inputs()

    def _L0_xattn_setup():
        import jax, jax.numpy as jnp
        import numpy as np
        B, S, D = (2, 256, 128)
        H = 16
        DH = D // H
        LAMBDA_INIT = 0.8
        EPS = 1e-05
        SCALE = 1.0 / np.sqrt(DH)
        key = jax.random.key(seed)
        ks = jax.random.split(key, 13)
        inp = {'query': jax.random.normal(ks[0], (B, S, D), jnp.float32), 'key': jax.random.normal(ks[1], (B, S, D), jnp.float32), 'value': jax.random.normal(ks[2], (B, S, D), jnp.float32), 'attn_mask': jnp.zeros((B, H, S, S), jnp.float32), 'W_q': jax.random.normal(ks[3], (D, 2 * DH * H), jnp.float32) * 0.02, 'W_k': jax.random.normal(ks[4], (D, 2 * DH * H), jnp.float32) * 0.02, 'W_v': jax.random.normal(ks[5], (D, DH * H), jnp.float32) * 0.02, 'W_o': jax.random.normal(ks[6], (DH * H, D), jnp.float32) * 0.02, 'lambda_q1': jax.random.normal(ks[7], (H, DH), jnp.float32) * 0.1, 'lambda_k1': jax.random.normal(ks[8], (H, DH), jnp.float32) * 0.1, 'lambda_q2': jax.random.normal(ks[9], (H, DH), jnp.float32) * 0.1, 'lambda_k2': jax.random.normal(ks[10], (H, DH), jnp.float32) * 0.1, 'rms_scale': jnp.ones((DH,), jnp.float32)}
        return inp
    _L0_xattn_all = _L0_xattn_setup()
    _L0_xattn_in = {k: v for k, v in _L0_xattn_all.items() if k in ('W_q', 'W_k', 'W_v', 'W_o', 'lambda_q1', 'lambda_k1', 'lambda_q2', 'lambda_k2', 'rms_scale')}
    del _L0_xattn_all

    def _L0_ffn_setup():
        import jax, jax.numpy as jnp
        import numpy as np
        DMODEL = 128
        N_EXPERTS = 32
        EXPERT_SIZE = 64
        N_HEADS = 4
        WEIGHT_SCALE = 1.0
        key = jax.random.key(seed)
        k0, k1, k2, k3 = jax.random.split(key, 4)
        x = jax.random.normal(k0, (2, 256, DMODEL), dtype=jnp.float32)
        expert_sel = jax.random.normal(k1, (N_EXPERTS, DMODEL), dtype=jnp.float32) * DMODEL ** (-0.5)
        keys = jax.random.normal(k2, (N_EXPERTS, DMODEL, EXPERT_SIZE), dtype=jnp.float32) * DMODEL ** (-0.5)
        values = jax.random.normal(k3, (N_EXPERTS, EXPERT_SIZE, DMODEL), dtype=jnp.float32) * (N_EXPERTS * EXPERT_SIZE) ** (-0.5)
        return {'x': x, 'expert_sel': expert_sel, 'keys': keys, 'values': values}
    _L0_ffn_all = _L0_ffn_setup()
    _L0_ffn_in = {k: v for k, v in _L0_ffn_all.items() if k in ('expert_sel', 'keys', 'values')}
    del _L0_ffn_all
    return {'x': x, 'ctx_1024': ctx_1024, 'mask_Bx16xSxS2_ff0': mask_Bx16xSxS2_ff0, 'L0_xattn_W_q': _L0_xattn_in['W_q'], 'L0_xattn_W_k': _L0_xattn_in['W_k'], 'L0_xattn_W_v': _L0_xattn_in['W_v'], 'L0_xattn_W_o': _L0_xattn_in['W_o'], 'L0_xattn_lambda_q1': _L0_xattn_in['lambda_q1'], 'L0_xattn_lambda_k1': _L0_xattn_in['lambda_k1'], 'L0_xattn_lambda_q2': _L0_xattn_in['lambda_q2'], 'L0_xattn_lambda_k2': _L0_xattn_in['lambda_k2'], 'L0_xattn_rms_scale': _L0_xattn_in['rms_scale'], 'L0_ffn_expert_sel': _L0_ffn_in['expert_sel'], 'L0_ffn_keys': _L0_ffn_in['keys'], 'L0_ffn_values': _L0_ffn_in['values']}

def reference(x, ctx_1024, mask_Bx16xSxS2_ff0, L0_xattn_W_q, L0_xattn_W_k, L0_xattn_W_v, L0_xattn_W_o, L0_xattn_lambda_q1, L0_xattn_lambda_k1, L0_xattn_lambda_q2, L0_xattn_lambda_k2, L0_xattn_rms_scale, L0_ffn_expert_sel, L0_ffn_keys, L0_ffn_values):
    import jax
    import jax.numpy as jnp

    def _L0_xattn_ref(query, key, value, attn_mask, W_q, W_k, W_v, W_o, lambda_q1, lambda_k1, lambda_q2, lambda_k2, rms_scale):
        import jax, jax.numpy as jnp
        import numpy as np
        B, S, D = (2, 256, 128)
        H = 16
        DH = D // H
        LAMBDA_INIT = 0.8
        EPS = 1e-05
        SCALE = 1.0 / np.sqrt(DH)
        b, s, _ = value.shape
        q = (query @ W_q).reshape(b, s, H, 2 * DH).transpose(0, 2, 1, 3)
        k = (key @ W_k).reshape(b, s, H, 2 * DH).transpose(0, 2, 1, 3)
        v = (value @ W_v).reshape(b, s, H, DH).transpose(0, 2, 1, 3)
        q1, q2 = (q[..., :DH], q[..., DH:])
        k1, k2 = (k[..., :DH], k[..., DH:])
        lam = jnp.exp(jnp.sum(lambda_q1 * lambda_k1, -1)) - jnp.exp(jnp.sum(lambda_q2 * lambda_k2, -1)) + LAMBDA_INIT
        lam = lam[None, :, None, None]
        s1 = jnp.einsum('bhqd,bhkd->bhqk', q1, k1) * SCALE + attn_mask
        s2 = jnp.einsum('bhqd,bhkd->bhqk', q2, k2) * SCALE + attn_mask
        attn = jax.nn.softmax(s1, axis=-1) - lam * jax.nn.softmax(s2, axis=-1)
        out = jnp.einsum('bhqk,bhkd->bhqd', attn, v)
        rms = jnp.sqrt(jnp.mean(out * out, axis=-1, keepdims=True) + EPS)
        out = out / rms * rms_scale
        out = out * (1.0 - LAMBDA_INIT)
        out = out.transpose(0, 2, 1, 3).reshape(b, s, H * DH)
        return out @ W_o

    def _L0_ffn_ref(x, expert_sel, keys, values):
        import jax, jax.numpy as jnp
        import numpy as np
        DMODEL = 128
        N_EXPERTS = 32
        EXPERT_SIZE = 64
        N_HEADS = 4
        WEIGHT_SCALE = 1.0
        B, S, D = x.shape
        xt = x.reshape(-1, D)
        N = xt.shape[0]
        sel_logits = jnp.einsum('nd,ed->ne', xt, expert_sel)
        gates = jax.nn.sigmoid(sel_logits)
        sel_val, sel_idx = jax.lax.top_k(gates, N_HEADS)
        gate_full = jnp.zeros_like(gates).at[jnp.arange(N)[:, None], sel_idx].set(sel_val)
        scores = jax.nn.relu(jnp.einsum('nd,edf->nef', xt, keys))
        scores = scores * gate_full[:, :, None]
        out = jnp.einsum('nef,efv->nv', scores, values)
        return out.reshape(B, S, -1)
    x = x + _L0_xattn_ref(_layernorm(x, axis=-1), ctx_1024, ctx_1024, mask_Bx16xSxS2_ff0, L0_xattn_W_q, L0_xattn_W_k, L0_xattn_W_v, L0_xattn_W_o, L0_xattn_lambda_q1, L0_xattn_lambda_k1, L0_xattn_lambda_q2, L0_xattn_lambda_k2, L0_xattn_rms_scale)
    x = x + _L0_ffn_ref(_layernorm(x, axis=-1), L0_ffn_expert_sel, L0_ffn_keys, L0_ffn_values)
    return x

_drawn_inputs = setup_inputs


def setup_inputs(seed=0):
    import zlib

    import numpy as np

    out = dict(_drawn_inputs(seed))
    spreads = {'L0_xattn_rms_scale': (1.0, 0.6)}
    factors = {'L0_xattn_W_q': 3.433,
     'L0_xattn_W_k': 3.575,
     'L0_xattn_lambda_q1': 8.0,
     'L0_xattn_lambda_k1': 8.0,
     'L0_xattn_lambda_q2': 8.0,
     'L0_xattn_lambda_k2': 8.0}
    for name, (base, spread) in spreads.items():
        noise = np.random.default_rng([zlib.crc32(name.encode()), seed]).standard_normal(out[name].shape)
        drawn = base * np.exp(spread * noise) if base else spread * noise
        out[name] = jnp.asarray(drawn.astype(out[name].dtype))
    for name, factor in factors.items():
        out[name] = (out[name] * factor).astype(out[name].dtype)
    return out
```

```python
from contextlib import ExitStack

import concourse.bass as bass
from concourse import mybir

ALU = mybir.AluOpType
ACT = mybir.ActivationFunctionType
AX = mybir.AxisListType
F32 = mybir.dt.float32
BF16 = mybir.dt.bfloat16
I32 = mybir.dt.int32

P = 128
B, S, D = 64, 64, 128
H, DH = 16, 8
E, F, TOPK = 32, 64, 4
LAMBDA_INIT = 0.8
EPS = 1e-5
QK_SCALE = DH ** -0.5
NT = B * S // P
NG = 4
NC = 8
TC = NT // NC
CW = TC * P
FT = E * F // P
EPT = P // F
RSQRT_MAGIC = float(0x5F3759DF)
HIDE = -3.0e38
NOMATCH = 3.0e38


def xattn_ffn(nc, x, ctx_in, mask, W_q, W_k, W_v, W_o, lq1, lk1, lq2, lk2, rms_scale,
              expert_sel, keys, values, out):
    with ExitStack() as stack:
        def sb(name, shape, dt=F32):
            return stack.enter_context(nc.sbuf_tensor(name, shape, dt))

        def sem(name):
            return stack.enter_context(nc.semaphore(name))

        ident = sb("ident", [P, P])
        ident_bf = sb("ident_bf", [P, P], BF16)
        head_cols = sb("head_cols", [P, NG])
        spread = sb("spread", [96, E * F], BF16)
        wq_raw = sb("wq_raw", [P, 2 * P])
        wk_raw = sb("wk_raw", [P, 2 * P])
        wq = sb("wq", [P, 2, P])
        wk = sb("wk", [P, 2, P])
        wv = sb("wv", [P, P])
        wo_raw = sb("wo_raw", [P, 2, D])
        wo = sb("wo", [P, 2, D])
        rms_col = sb("rms_col", [P, 1])
        rms_scaled = sb("rms_scaled", [P, 1])
        sel_rows = sb("sel_rows", [E, D])
        sel_t = sb("sel_t", [P, E])
        keys_sb = sb("keys_sb", [P, E * F])
        values_sb = sb("values_sb", [P, FT, D])
        lam_in = sb("lam_in", [P, 4, H * DH])
        lam_prod = sb("lam_prod", [P, 2, H * DH])
        lam_sum = sb("lam_sum", [P, 2, H])
        lam_exp = sb("lam_exp", [P, 2, H])
        lam_all = sb("lam_all", [P, H])
        lam = sb("lam", [P, 2, 8])

        x_all = sb("x_all", [P, NT, D])
        os_all = sb("os_all", [P, NT, 288])
        stats = sb("stats", [P, NT, 6])
        st_a = sb("st_a", [P, NT])
        st_b = sb("st_b", [P, NT])
        mean = sb("mean", [P, NT])
        rstd = sb("rstd", [P, NT])

        mask_sb = [sb(f"mask_sb{e}", [P, NG, 2, 2, S]) for e in range(2)]
        ctx_sb = [sb(f"ctx_sb{e}", [P, D]) for e in range(2)]
        xn = [sb(f"xn{e}", [P, D]) for e in range(2)]
        xn_t = [sb(f"xn_t{e}", [P, P]) for e in range(2)]
        ctx_t = [sb(f"ctx_t{e}", [P, 2, 2, S]) for e in range(2)]
        q_t = [sb(f"q_t{e}", [P, 2, P]) for e in range(2)]
        k_t = [sb(f"k_t{e}", [P, 2, P]) for e in range(2)]
        qm = [sb(f"qm{e}", [P, 2, 2, NG, S]) for e in range(2)]
        v2 = [sb(f"v2{e}", [P, 2, 8, 36]) for e in range(2)]
        prob = [sb(f"prob{r}", [P, 4, 2, S]) for r in range(4)]
        prob_t = [sb(f"prob_t{r}", [P, 4, P]) for r in range(2)]
        rowmax = sb("rowmax", [P, 2, 8])

        linv = sb("linv", [P, 64, 2])
        om = sb("om", [P, 64, 2, 8])
        oc = sb("oc", [P, 64, 8])
        osq = sb("osq", [P, 64, 8])
        on = sb("on", [P, 64, 8])
        v_a = sb("v_a", [P, 64])
        v_b = sb("v_b", [P, 64])
        v_c = sb("v_c", [P, 64])
        o_t = sb("o_t", [P, CW])
        fstats = sb("fstats", [P, TC, 6])
        fmean = sb("fmean", [P, TC])
        f_a = sb("f_a", [P, TC])
        f_b = sb("f_b", [P, TC])
        f_c = sb("f_c", [P, TC])
        fn = sb("fn", [P, TC, D])
        fn_t = [sb(f"fn_t{r}", [P, CW]) for r in range(2)]
        logit = sb("logit", [P, TC, E])
        eneg = sb("eneg", [P, TC, E])
        top8 = sb("top8", [P, TC, 8])
        rest = sb("rest", [P, TC, E])
        gate = sb("gate", [P, TC, E])
        gpart = sb("gpart", [P, TC, 3, E], BF16)
        gate_t = [sb(f"gate_t{r}", [96, CW], BF16) for r in range(2)]
        hid = [sb(f"hid{r}", [P, CW]) for r in range(3)]
        ghid = [sb(f"ghid{r}", [P, CW]) for r in range(3)]
        y_t = sb("y_t", [P, CW])
        y_sb = [sb(f"y_sb{r}", [P, TC, D]) for r in range(2)]

        bank = [stack.enter_context(nc.psum_tensor(f"bank{r}", [P, 512], F32)) for r in range(8)]
        sc_ps, pt_ps, o_ps, m_ps, m2_ps = bank[0:2], bank[2:4], bank[4:6], bank[6], bank[7]
        h_ps, g_ps, y_ps, t_ps, w_ps = bank[0:2], bank[2:4], bank[4], bank[5], bank[6:8]

        x_in = sem("x_in")
        w_in = sem("w_in")
        w2_in = sem("w2_in")
        wp_in = sem("wp_in")
        mask_in = [sem(f"mask_in{e}") for e in range(2)]
        ctx_in_s = [sem(f"ctx_in{e}") for e in range(2)]
        ident0 = sem("ident0")
        ident_ok = sem("ident_ok")
        dve_own = sem("dve_own")
        heads_ok = sem("heads_ok")
        consts_ok = sem("consts_ok")
        w_perm = sem("w_perm")
        rms_ok = sem("rms_ok")
        lam_sums = sem("lam_sums")
        lam_exps = sem("lam_exps")
        v2_init = sem("v2_init")
        stat_done = sem("stat_done")
        seltr = sem("seltr")
        xn_ready = sem("xn_ready")
        tr_done = sem("tr_done")
        xt_ready = sem("xt_ready")
        qk_done = sem("qk_done")
        vp_done = sem("vp_done")
        q_out = sem("q_out")
        k_out = sem("k_out")
        v_out = sem("v_out")
        qm_ready = sem("qm_ready")
        scored = sem("scored")
        masked = sem("masked")
        maxed = sem("maxed")
        shifted = sem("shifted")
        exped = sem("exped")
        turned = sem("turned")
        turned_out = sem("turned_out")
        pv_done = sem("pv_done")
        o_out_a = sem("o_out_a")
        o_out_v = sem("o_out_v")
        post_v = sem("post_v")
        post_p = sem("post_p")
        post_e = sem("post_e")
        post_a = sem("post_a")
        h_done = sem("h_done")
        g_done = sem("g_done")
        relu_done = sem("relu_done")
        gated = sem("gated")
        acc_done = sem("acc_done")
        used = sem("used")
        y_out = sem("y_out")
        y_turned = sem("y_turned")
        y_sum = sem("y_sum")
        stored = [sem(f"stored{r}") for r in range(2)]

        x_v = x.rearrange("b s d -> (b s) d").rearrange("(i p) d -> p i d", p=P)
        out_v = out.rearrange("b s d -> (b s) d").rearrange("(i p) d -> p i d", p=P)
        ctx_v = ctx_in.rearrange("b s d -> (b s) d").rearrange("(i p) d -> p i d", p=P)
        mask_v = mask.rearrange("b (n j) q k -> (j q) b n k", j=2)

        N_W = 16 * 3
        N_W2 = 16 * 4
        N_WP = 16 * (16 + 16 + 3)

        block = stack.enter_context(nc.Block())

        @block.sync
        def _(sp):
            def load_mask(i, e):
                for b in range(2):
                    sp.dma_start(mask_sb[e][:, :, :, b, :].rearrange("p g r k -> p (g r) k"), mask_v[:, 2 * i + b]).then_inc(mask_in[e], 16)

            def load_ctx(i, e):
                sp.dma_start(ctx_sb[e][:, :], ctx_v[:, i, :]).then_inc(ctx_in_s[e], 16)

            for c in range(4):
                sp.dma_start(x_all[:, 8 * c:8 * c + 8, :], x_v[:, 8 * c:8 * c + 8, :]).then_inc(x_in, 16)
            sp.dma_start(wq_raw[:, :], W_q).then_inc(w_in, 16)
            sp.dma_start(wk_raw[:, :], W_k).then_inc(w_in, 16)
            sp.dma_start(wv[:, :], W_v).then_inc(w_in, 16)
            load_ctx(0, 0)
            load_mask(0, 0)
            load_ctx(1, 1)
            load_mask(1, 1)
            for a in range(4):
                src = (lq1, lk1, lq2, lk2)[a].rearrange("(o h) d -> o (h d)", o=1)
                sp.dma_start(lam_in[:, a, :], src.to_broadcast([P, H * DH])).then_inc(w2_in, 16)

            def reload(i, e):
                sp.wait_ge(tr_done, i - 1)
                load_ctx(i, e)
                sp.wait_ge(masked, NG * (i - 1))
                load_mask(i, e)

            reload(2, 0)
            reload(3, 1)
            with sp.Fori(2, NT // 2) as t:
                reload(2 * t, 0)
                reload(2 * t + 1, 1)
            for r in range(2):
                sp.wait_ge(stored[r], 16 * (NC // 2))

        @block.gpsimd
        def _(pool):
            nc.gpsimd.memset(ident[:, :], 0.0).then_inc(ident0, 1)
            pool.wait_ge(ident0, 1)
            nc.gpsimd.affine_select(out=ident[:, :], in_=ident[:, :], compare_op=ALU.not_equal, fill=1.0,
                                    base=0, pattern=[[-1, P]], channel_multiplier=1).then_inc(ident_ok, 1)
            for b in range(2):
                for hp in range(8):
                    r0 = 64 * b + 8 * hp
                    src = W_o.rearrange("(hp j d) n -> hp d j n", j=2, d=DH)[hp]
                    pool.dma_start(wo_raw[r0:r0 + 8, :, :], src).then_inc(wp_in, 16)
            for r in range(16):
                pool.dma_start(rms_col[8 * r:8 * r + 8, :], rms_scale.rearrange("(d o) -> d o", o=1)).then_inc(wp_in, 16)
            pool.dma_start(sel_rows[:, :], expert_sel).then_inc(wp_in, 16)
            pool.dma_start(keys_sb[:, :].rearrange("d (e f) -> d e f", e=E),
                           keys.rearrange("e d f -> d e f")).then_inc(wp_in, 16)
            pool.dma_start(values_sb[:, :, :], values.rearrange("(t e) f d -> (e f) t d", e=EPT)).then_inc(wp_in, 16)
            pool.wait_ge(heads_ok, 1)

            def one_head(i, e, first):
                pool.wait_ge(q_out, i + 1)
                if not first:
                    pool.wait_ge(scored, NG * (i - 1))
                pool.nop(nofuse=True)
                for j in range(NG):
                    nc.gpsimd.tensor_scalar(qm[e][:, :, :, j, :].rearrange("p h b s -> p (h b) s"),
                                            q_t[e][:, :, :].rearrange("p h (b s) -> p (h b) s", b=2), head_cols[:, j:j + 1], None,
                                            ALU.mult).then_inc(qm_ready, 1)

            one_head(0, 0, True)
            one_head(1, 1, True)
            with pool.Fori(1, NT // 2) as t:
                one_head(2 * t, 0, False)
                one_head(2 * t + 1, 1, False)

            def post(c):
                pool.wait_ge(post_v, 6 * c + 1)
                if not isinstance(c, int) or c:
                    pool.wait_ge(post_p, 4 * c)
                os_c = os_all[:, bass.ts(c, TC), :].rearrange("p i (n v) -> p (i n) v", v=9)
                nc.gpsimd.tensor_tensor(om[:, :, :, :].rearrange("p n h v -> p (n h) v"), os_c[:, :, 0:8],
                                        linv[:, :, :].rearrange("p n h -> p (n h)").unsqueeze(2).to_broadcast([P, P, 8]),
                                        ALU.mult).then_inc(post_p, 1)
                pool.wait_ge(post_p, 4 * c + 1)
                nc.gpsimd.tensor_tensor(oc[:, :, :], om[:, :, 0, :], om[:, :, 1, :], ALU.subtract).then_inc(post_p, 1)
                pool.wait_ge(post_p, 4 * c + 2)
                nc.gpsimd.tensor_tensor(osq[:, :, :], oc[:, :, :], oc[:, :, :], ALU.mult).then_inc(post_p, 1)
                pool.wait_ge(post_v, 6 * c + 2)
                nc.gpsimd.tensor_tensor(on[:, :, :], oc[:, :, :],
                                        v_a[:, :].unsqueeze(2).to_broadcast([P, 64, 8]),
                                        ALU.mult).then_inc(post_p, 1)

            post(0)
            with pool.Fori(1, NC) as c:
                post(c)

        @block.tensor
        def _(pe):
            def pre_turn_t(i, e, nth, first):
                pe.wait_ge(xn_ready, i + 1)
                pe.wait_ge(ctx_in_s[e], 16 * nth)
                if not first:
                    pe.wait_ge(v_out, 2 * i)
                pe.transpose(m_ps[:, 0:P], xn[e][:, :], ident[:, :])
                pe.transpose(m_ps[:, P:2 * P], ctx_sb[e][:, :], ident[:, :]).then_inc(tr_done, 1)

            def project(i, e, first):
                pe.wait_ge(xt_ready, 2 * i + 2)
                if not first:
                    pe.wait_ge(k_out, i)
                    pe.wait_ge(q_out, i)
                for h in range(2):
                    pe.matmul(m2_ps[:, h * P:(h + 1) * P], wq[:, h, :], xn_t[e][:, :], start=(h == 0), stop=True,
                              skip_group_check=True)
                for h in range(2):
                    mm = pe.matmul(m2_ps[:, (2 + h) * P:(3 + h) * P], wk[:, h, :], ctx_t[e][:, :, 0, :],
                                   start=False, stop=True, skip_group_check=True)
                mm.then_inc(qk_done, 1)
                for b in range(2):
                    mm = pe.matmul(m_ps[:, (2 + b) * P:(3 + b) * P],
                                   ctx_t[e][:, b, :, :].rearrange("p u s -> p (u s)"), wv[:, :],
                                   start=(b == 0), stop=True, skip_group_check=True)
                mm.then_inc(vp_done, 1)

            def scores(i, e, g, fresh):
                n = NG * i + g
                if g == 0:
                    pe.wait_ge(qm_ready, NG * i + NG)
                    pe.wait_ge(k_out, i + 1)
                if fresh < 0:
                    pe.wait_ge(masked, n - 1)
                rows = slice(32 * g, 32 * g + 32)
                for b in range(2):
                    for p in range(2):
                        for h in range(2):
                            o = ((p * 2 + b) * 2 + h) * S
                            mm = pe.matmul(sc_ps[g % 2][:, o:o + S],
                                           qm[e][rows, h, b, 2 * p:2 * p + 2, :].rearrange("p j s -> p (j s)"),
                                           k_t[e][rows, h, b * S:b * S + S],
                                           start=(o == 0), stop=True, skip_group_check=True)
                mm.then_inc(scored, 1)

            def turn(i, e, g, first):
                n = NG * i + g
                pe.wait_ge(exped, n + 1)
                if not first:
                    pe.wait_ge(turned_out, n - 1)
                for a in range(4):
                    mm = pe.transpose(pt_ps[g % 2][:, a * P:(a + 1) * P],
                                      prob[g][:, a, :, :].rearrange("p h k -> p (h k)"), ident[:, :])
                mm.then_inc(turned, 1)

            def attend(i, e, g, first):
                n = NG * i + g
                pe.wait_ge(turned_out, n + 1)
                if g == 0:
                    pe.wait_ge(v_out, 2 * i + 2)
                if g % 2 == 0 and not first:
                    pe.wait_ge(o_out_a, 2 * i + g // 2 - 1)
                    pe.wait_ge(o_out_v, 2 * i + g // 2 - 1)
                for b in range(2):
                    for p in range(2):
                        o = (b * 4 + (g % 2) * 2 + p) * 36
                        mm = pe.matmul(o_ps[g // 2][:, o:o + 36], prob_t[g % 2][:, p * 2 + b, :],
                                       v2[e][:, b, 2 * g + p, :], start=(g % 2 == 0 and b == 0 and p == 0),
                                       stop=True, skip_group_check=True)
                mm.then_inc(pv_done, 1)

            def tile_steps(t, e, peel_first, peel_last):
                i = 2 * t + e
                f = peel_first and e == 0
                f2 = peel_first and e == 1
                nxt_nth = t + 1 if e == 0 else t + 2
                for g in range(NG):
                    scores(i, e, g, 1 if (f and g < 2) else -1)
                    if g >= 2:
                        turn(i, e, g - 2, f)
                    elif not f:
                        turn(i - 1, 1 - e, g + 2, False)
                    if not (peel_last and e == 1):
                        if g == 0:
                            pre_turn_t(i + 1, 1 - e, nxt_nth, False)
                        if g == 1:
                            project(i + 1, 1 - e, False)
                    if g == 3:
                        attend(i, e, 0, f)
                    elif not f:
                        attend(i - 1, 1 - e, g + 1, f2 and g < 2)

            pe.wait_ge(ident_ok, 1)
            pe.wait_ge(wp_in, N_WP)
            pe.transpose(m2_ps[:, 0:E], sel_rows[:, :], ident[0:E, 0:E]).then_inc(seltr, 1)
            pe.wait_ge(w_perm, 6)
            pe.wait_ge(w_in, N_W)
            pre_turn_t(0, 0, 1, True)
            project(0, 0, True)
            tile_steps(0, 0, True, False)
            tile_steps(0, 1, True, False)
            with pe.Fori(1, NT // 2 - 1) as t:
                tile_steps(t, 0, False, False)
                tile_steps(t, 1, False, False)
            tile_steps(NT // 2 - 1, 0, False, False)
            tile_steps(NT // 2 - 1, 1, False, True)
            L = NT - 1
            turn(L, 1, 2, False)
            attend(L, 1, 1, False)
            turn(L, 1, 3, False)
            attend(L, 1, 2, False)
            attend(L, 1, 3, False)

            def post_o(c):
                pe.wait_ge(post_p, 4 * c + 4)
                if isinstance(c, int) and c == 0:
                    pe.wait_ge(o_out_a, 2 * NT)
                    pe.wait_ge(o_out_v, 2 * NT)
                    pe.wait_ge(v_out, 2 * NT)
                    pe.wait_ge(k_out, NT)
                    pe.wait_ge(q_out, NT)
                for ii in range(TC):
                    src = on[:, 16 * ii:16 * ii + 16, :].rearrange("p n v -> p (n v)")
                    mm = pe.transpose(t_ps[:, ii * P:(ii + 1) * P], src, ident[:, :])
                mm.then_inc(post_e, 1)

            def post_w(c):
                pe.wait_ge(post_a, 5 * c + 1)
                if not isinstance(c, int) or c >= 2:
                    pe.wait_ge(y_sum, c - 1)
                pe.nop(nofuse=True)
                for b in range(2):
                    r = slice(64 * b, 64 * b + 64)
                    for ii in range(TC):
                        for j in range(2):
                            mm = pe.matmul(w_ps[b][r, ii * P:(ii + 1) * P],
                                           o_t[r, ii * P + 64 * j:ii * P + 64 * j + 64], wo[r, j, :],
                                           start=(j == 0 and ii == 0), stop=(j == 1), skip_group_check=True)
                mm.then_inc(post_e, 1)

            def post_n(c):
                pe.wait_ge(post_v, 6 * c + 4)
                for ii in range(TC):
                    mm = pe.transpose(t_ps[:, ii * P:(ii + 1) * P], fn[:, ii, :], ident[:, :])
                mm.then_inc(post_e, 1)

            def post_l(c, r):
                pe.wait_ge(post_a, 5 * c + 2)
                for ii in range(TC):
                    mm = pe.matmul(t_ps[:, ii * E:(ii + 1) * E], fn_t[r][:, ii * P:(ii + 1) * P], sel_t[:, :],
                                   start=(ii == 0), stop=True, skip_group_check=True)
                mm.then_inc(post_e, 1)

            def post_g(c):
                pe.wait_ge(post_v, 6 * c + 6)
                tb = t_ps[:, :].bitcast(BF16)
                for ii in range(TC):
                    mm = pe.transpose(tb[0:96, ii * P:(ii + 1) * P],
                                      gpart[:, ii, :, :].rearrange("p a e -> p (a e)"), ident_bf[:, :])
                mm.then_inc(post_e, 1)

            def hidden(c, r, f, first):
                n = FT * c + f
                if f == 0:
                    pe.wait_ge(post_a, 5 * c + 5)
                if not first:
                    pe.wait_ge(relu_done, n - 1)
                pe.matmul(h_ps[f % 2][:, :], keys_sb[:, f * P:(f + 1) * P], fn_t[r][:, :], start=True,
                          stop=True).then_inc(h_done, 1)
                if not first:
                    pe.wait_ge(gated, n - 1)
                pe.matmul(g_ps[f % 2][:, :], spread[:, f * P:(f + 1) * P], gate_t[r][:, :], start=True,
                          stop=True).then_inc(g_done, 1)

            def down(c, f):
                n = FT * c + f
                pe.wait_ge(gated, n + 1)
                if f == 0 and (not isinstance(c, int) or c):
                    pe.wait_ge(y_out, c)
                mm = pe.matmul(y_ps[:, :], values_sb[:, f, :], ghid[(f) % 2][:, :],
                               start=(f == 0), stop=(f == FT - 1))
                mm.then_inc(used, 1)

            def finish(c):
                pe.wait_ge(y_out, c + 1)
                if not isinstance(c, int) or c < NC - 1:
                    pe.wait_ge(post_v, 6 * c + 9)
                for ii in range(TC):
                    mm = pe.transpose(w_ps[0][:, ii * P:(ii + 1) * P], y_t[:, ii * P:(ii + 1) * P], ident[:, :])
                mm.then_inc(y_turned, 1)

            def chunk(c, r, first, last):
                for f in range(FT):
                    hidden(c, r, f, first and f < 2)
                    if f >= 2:
                        down(c, f - 2)
                    if f == 2 and not first:
                        finish(c - 1)
                    if not last:
                        if f == 5:
                            post_o(c + 1)
                        if f == 7:
                            post_w(c + 1)
                        if f == 10:
                            post_n(c + 1)
                        if f == 11:
                            post_l(c + 1, 1 - r)
                        if f == 15:
                            post_g(c + 1)
                down(c, FT - 2)
                down(c, FT - 1)

            post_o(0)
            post_w(0)
            post_n(0)
            post_l(0, 0)
            post_g(0)
            chunk(0, 0, True, False)
            with pe.Fori(0, (NC - 2) // 2) as u:
                chunk(2 * u + 1, 1, False, False)
                chunk(2 * u + 2, 0, False, False)
            chunk(NC - 1, 1, False, True)
            finish(NC - 1)

        @block.scalar
        def _(act):
            act.wait_ge(w_in, N_W)
            for raw, w in ((wq_raw, wq), (wk_raw, wk)):
                for h in range(2):
                    src = raw[:, :].rearrange("p (n a d) -> p n a d", n=H, a=2)[:, :, h, :]
                    nc.scalar.copy(w[:, h, :].rearrange("p (n d) -> p n d", n=H), src).then_inc(w_perm, 1)
            act.wait_ge(wp_in, N_WP)
            nc.scalar.mul(rms_scaled[:, :], rms_col[:, :], 1.0 - LAMBDA_INIT).then_inc(rms_ok, 1)
            act.wait_ge(rms_ok, 1)
            nc.scalar.activation(wo[:, :, :], wo_raw[:, :, :], ACT.Copy, scale=rms_scaled[:, 0:1]).then_inc(w_perm, 1)
            act.wait_ge(seltr, 1)
            nc.scalar.copy(sel_t[:, :], m2_ps[:, 0:E]).then_inc(w_perm, 1)
            act.wait_ge(lam_sums, 1)
            nc.scalar.activation(lam_exp[:, :, :], lam_sum[:, :, :], ACT.Exp).then_inc(lam_exps, 1)

            def pre_turn_out(i, e, first):
                act.wait_ge(tr_done, i + 1)
                if not first:
                    act.wait_ge(vp_done, i - 1)
                nc.scalar.copy(xn_t[e][:, :], m_ps[:, 0:P]).then_inc(xt_ready, 1)
                src = m_ps[:, P:2 * P].rearrange("p (b s) -> p b s", b=2).unsqueeze(2).to_broadcast([P, 2, 2, S])
                nc.scalar.copy(ctx_t[e][:, :, :, :], src).then_inc(xt_ready, 1)

            def project_out(i, e, first):
                act.wait_ge(qk_done, i + 1)
                if not first:
                    act.wait_ge(qm_ready, NG * (i - 1))
                    act.wait_ge(scored, NG * (i - 1))
                nc.scalar.mul(q_t[e][:, :, :].rearrange("p h t -> p (h t)"), m2_ps[:, 0:2 * P], QK_SCALE).then_inc(q_out, 1)
                nc.scalar.copy(k_t[e][:, :, :].rearrange("p h t -> p (h t)"), m2_ps[:, 2 * P:4 * P]).then_inc(k_out, 1)
                act.wait_ge(vp_done, i + 1)
                if first:
                    act.wait_ge(v2_init, 4)
                else:
                    act.wait_ge(pv_done, NG * (i - 1))
                for h in range(2):
                    r = slice(64 * h, 64 * h + 64)
                    src = m_ps[r, 2 * P:4 * P].rearrange("p (n j d) -> p n j d", j=2, d=DH)
                    dst = v2[e][r, :, :, :].rearrange("p b n (j h v) -> p (b n) j h v", j=2, h=2)[:, :, :, h, 0:8]
                    nc.scalar.copy(dst, src).then_inc(v_out, 1)

            def exponent(i, g):
                n = NG * i + g
                act.wait_ge(shifted, n + 1)
                pr = prob[g][:, :, :, :].rearrange("p a h k -> p (a h k)")
                nc.scalar.activation(pr, pr, ACT.Exp).then_inc(exped, 1)

            def turn_out(i, g, first):
                n = NG * i + g
                act.wait_ge(turned, n + 1)
                if not first:
                    act.wait_ge(pv_done, n - 1)
                nc.scalar.copy(prob_t[g % 2][:, :, :].rearrange("p a k -> p (a k)"), pt_ps[g % 2][:, :]).then_inc(turned_out, 1)

            def sums_out(i, m):
                act.wait_ge(pv_done, NG * i + 2 * m + 2)
                src = o_ps[m][0:64, 0:288].rearrange("p (b n v) -> p b n v", b=2, v=36)[:, :, :, 0:18]
                dst = os_all[0:64, bass.ds(i, 1), :].rearrange("p i (b m n v) -> p (i b) m n v", b=2, m=2, n=4)[:, :, m, :, :]
                nc.scalar.copy(dst, src).then_inc(o_out_a, 1)

            def tile_steps(t, e, peel_first, peel_last):
                i = 2 * t + e
                f = peel_first and e == 0
                for g in range(NG):
                    if not (peel_last and e == 1):
                        if g == 1:
                            pre_turn_out(i + 1, 1 - e, f)
                        if g == 2:
                            project_out(i + 1, 1 - e, f)
                    exponent(i, g)
                    if g >= 1:
                        turn_out(i, g - 1, f and g < 3)
                    elif not f:
                        turn_out(i - 1, 3, False)
                    if g == 1 and not f:
                        sums_out(i - 1, 1)
                    if g == 3:
                        sums_out(i, 0)

            pre_turn_out(0, 0, True)
            project_out(0, 0, True)
            tile_steps(0, 0, True, False)
            tile_steps(0, 1, True, False)
            with act.Fori(1, NT // 2 - 1) as t:
                tile_steps(t, 0, False, False)
                tile_steps(t, 1, False, False)
            tile_steps(NT // 2 - 1, 0, False, False)
            tile_steps(NT // 2 - 1, 1, False, True)
            turn_out(NT - 1, 3, False)
            sums_out(NT - 1, 1)

            def post_o(c):
                act.wait_ge(post_e, 5 * c + 1)
                nc.scalar.copy(o_t[:, :], t_ps[:, :]).then_inc(post_a, 1)

            def post_n(c, r):
                act.wait_ge(post_e, 5 * c + 3)
                if not isinstance(c, int) or c >= 2:
                    act.wait_ge(h_done, FT * (c - 1))
                nc.scalar.copy(fn_t[r][:, :], t_ps[:, :]).then_inc(post_a, 1)

            def post_l(c):
                act.wait_ge(post_e, 5 * c + 4)
                src = t_ps[:, 0:TC * E]
                nc.scalar.activation(eneg[:, :, :].rearrange("p i e -> p (i e)"), src, ACT.Exp, scale=-1.0).then_inc(post_a, 1)
                nc.scalar.copy(logit[:, :, :].rearrange("p i e -> p (i e)"), src).then_inc(post_a, 1)

            def post_g(c, r):
                act.wait_ge(post_e, 5 * c + 5)
                if not isinstance(c, int) or c >= 2:
                    act.wait_ge(g_done, FT * (c - 1))
                nc.scalar.copy(gate_t[r][:, :], t_ps[:, :].bitcast(BF16)[0:96, 0:CW]).then_inc(post_a, 1)

            def relu(c, f, first):
                n = FT * c + f
                act.wait_ge(h_done, n + 1)
                if not first:
                    act.wait_ge(gated, n - 1)
                nc.scalar.activation(hid[f % 2][:, :], h_ps[f % 2][:, :], ACT.Relu).then_inc(relu_done, 1)

            def y_copy(c):
                act.wait_ge(used, FT * c + FT)
                if not isinstance(c, int) or c:
                    act.wait_ge(y_turned, c)
                nc.scalar.copy(y_t[:, :], y_ps[:, :]).then_inc(y_out, 1)

            def store(c, r):
                act.wait_ge(y_sum, c + 1)
                act.dma_start(out_v[:, bass.ts(c, TC), :], y_sb[r][:, :, :]).then_inc(stored[r], 16)

            def chunk(c, r, first, last):
                for f in range(FT):
                    relu(c, f, first and f < 2)
                    if f == 0 and not first:
                        y_copy(c - 1)
                    if f == 5 and not first:
                        store(c - 1, 1 - r)
                    if not last:
                        if f == 6:
                            post_o(c + 1)
                        if f == 11:
                            post_n(c + 1, 1 - r)
                        if f == 12:
                            post_l(c + 1)
                if not last:
                    post_g(c + 1, 1 - r)

            post_o(0)
            post_n(0, 0)
            post_l(0)
            post_g(0, 0)
            chunk(0, 0, True, False)
            with act.Fori(0, (NC - 2) // 2) as u:
                chunk(2 * u + 1, 1, False, False)
                chunk(2 * u + 2, 0, False, False)
            chunk(NC - 1, 1, False, True)
            y_copy(NC - 1)
            store(NC - 1, 1)

        @block.vector
        def _(dve):
            own = [0]

            def step(ins):
                own[0] += 1
                ins.then_inc(dve_own, 1)
                dve.wait_ge(dve_own, own[0])

            for e in range(2):
                step(nc.vector.memset(v2[e][:, :, :, :], 0.0))
                for h in range(2):
                    r = slice(64 * h, 64 * h + 64)
                    ones = v2[e][r, :, :, :].rearrange("p b n (j h v) -> p (b n) j h v", j=2, h=2)[:, :, :, h, 8:9]
                    nc.vector.memset(ones, 1.0).then_inc(v2_init, 1)
            dve.wait_ge(ident_ok, 1)
            nc.vector.tensor_reduce(head_cols[:, :], ident[:, :].rearrange("p (g j d) -> p j g d", g=NG, j=NG),
                                    AX.XY, ALU.add).then_inc(heads_ok, 1)
            nc.vector.tensor_copy(ident_bf[:, :], ident[:, :]).then_inc(consts_ok, 1)
            for a in range(3):
                r = slice(32 * a, 32 * a + 32)
                nc.vector.tensor_copy(spread[r, :].rearrange("p (e f) -> p e f", e=E),
                                      ident[r, r].unsqueeze(2).to_broadcast([E, E, F])).then_inc(consts_ok, 1)
            dve.wait_ge(w2_in, N_W2)
            for a in range(2):
                step(nc.vector.tensor_tensor(lam_prod[:, a, :], lam_in[:, 2 * a, :], lam_in[:, 2 * a + 1, :], ALU.mult))
            nc.vector.tensor_reduce(lam_sum[:, :, :].rearrange("p a h -> p (a h)"),
                                    lam_prod[:, :, :].rearrange("p a (h d) -> p (a h) d", d=DH),
                                    AX.X, ALU.add).then_inc(lam_sums, 1)

            def rsqrt(v, y, w, n, mul, add):
                step(nc.vector.tensor_scalar(v, v, mul, add, ALU.mult, ALU.add))
                step(nc.vector.tensor_scalar(y.bitcast(I32), v.bitcast(I32), 1, None, ALU.logical_shift_right))
                step(nc.vector.tensor_scalar(y.bitcast(I32), y.bitcast(I32), -1.0, RSQRT_MAGIC, ALU.mult, ALU.add))
                for _ in range(3):
                    step(nc.vector.tensor_tensor(w, y, y, ALU.mult))
                    step(nc.vector.tensor_tensor(w, w, v, ALU.mult))
                    step(nc.vector.tensor_scalar(w, w, -0.5, 1.5, ALU.mult, ALU.add))
                    step(nc.vector.tensor_tensor(y, y, w, ALU.mult))

            dve.wait_ge(x_in, 64)
            with dve.Fori(0, NT) as i:
                nc.vector.bn_stats(stats[:, i, :], x_all[:, i, :]).then_inc(stat_done, 1)
            dve.wait_ge(stat_done, NT)

            def moments(st, mn, var, tmp):
                step(nc.vector.tensor_tensor(mn, st[:, :, 1], st[:, :, 4], ALU.add))
                step(nc.vector.tensor_tensor(tmp, st[:, :, 1], st[:, :, 4], ALU.subtract))
                step(nc.vector.tensor_tensor(tmp, tmp, tmp, ALU.mult))
                step(nc.vector.tensor_tensor(var, st[:, :, 2], st[:, :, 5], ALU.add))
                step(nc.vector.scalar_tensor_tensor(out=var, in0=tmp, scalar=float(D) / 4, in1=var,
                                                    op0=ALU.mult, op1=ALU.add))
                step(nc.vector.tensor_scalar(mn, mn, 0.5, None, ALU.mult))

            moments(stats, mean[:, :], st_a[:, :], st_b[:, :])
            rsqrt(st_a[:, :], rstd[:, :], st_b[:, :], NT, 1.0 / D, EPS)

            def norm_x(i, e, first):
                if not first:
                    dve.wait_ge(tr_done, i - 1)
                nc.vector.tensor_scalar(xn[e][:, :], x_all[:, i, :], mean[:, bass.ds(i, 1)], rstd[:, bass.ds(i, 1)],
                                        ALU.subtract, ALU.mult).then_inc(xn_ready, 1)

            norm_x(0, 0, True)
            dve.wait_ge(lam_exps, 1)
            step(nc.vector.tensor_tensor(lam_all[:, :], lam_exp[:, 0, :], lam_exp[:, 1, :], ALU.subtract))
            step(nc.vector.tensor_scalar(lam_all[:, :], lam_all[:, :], LAMBDA_INIT, None, ALU.add))
            for j in range(2):
                r = slice(64 * j, 64 * j + 64)
                src = lam_all[r, :].rearrange("p (n j) -> p n j", j=2)[:, :, j]
                for b in range(2):
                    step(nc.vector.tensor_copy(lam[r, b, :], src))

            def add_mask(i, e, g, nth, first):
                n = NG * i + g
                dve.wait_ge(scored, n + 1)
                if g == 0:
                    dve.wait_ge(mask_in[e], 32 * nth)
                if not first:
                    dve.wait_ge(turned, n - 3)
                nc.vector.tensor_tensor(prob[g][:, :, :, :], sc_ps[g % 2][:, :].rearrange("p (a h k) -> p a h k", a=4, h=2),
                                        mask_sb[e][:, g, :, :, :].rearrange("p r b k -> p (r b) k").unsqueeze(2).to_broadcast([P, 4, 2, S]),
                                        ALU.add).then_inc(masked, 1)

            def row_max(i, g):
                n = NG * i + g
                dve.wait_ge(masked, n + 1)
                nc.vector.tensor_reduce(rowmax[:, g % 2, :], prob[g][:, :, :, :].rearrange("p a h k -> p (a h) k"),
                                        AX.X, ALU.max).then_inc(maxed, 1)

            def shift(i, g):
                n = NG * i + g
                dve.wait_ge(maxed, n + 1)
                pr = prob[g][:, :, :, :].rearrange("p a h k -> p (a h) k")
                nc.vector.tensor_tensor(pr, pr, rowmax[:, g % 2, :].unsqueeze(2).to_broadcast([P, 8, S]),
                                        ALU.subtract).then_inc(shifted, 1)

            def sums_out(i, m):
                dve.wait_ge(pv_done, NG * i + 2 * m + 2)
                src = o_ps[m][64:128, 0:288].rearrange("p (b n v) -> p b n v", b=2, v=36)[:, :, :, 18:36]
                dst = os_all[64:128, bass.ds(i, 1), :].rearrange("p i (b m n v) -> p (i b) m n v", b=2, m=2, n=4)[:, :, m, :, :]
                nc.vector.tensor_copy(dst, src).then_inc(o_out_v, 1)

            def tile_steps(t, e, peel_first, peel_last):
                i = 2 * t + e
                f = peel_first and e == 0
                for g in range(NG):
                    add_mask(i, e, g, t + 1, f)
                    row_max(i, g)
                    if g == 0 and not (peel_last and e == 1):
                        norm_x(i + 1, 1 - e, f)
                    shift(i, g)
                    if g == 0 and not f:
                        sums_out(i - 1, 0)
                    if g == 2 and not f:
                        sums_out(i - 1, 1)

            tile_steps(0, 0, True, False)
            tile_steps(0, 1, True, False)
            with dve.Fori(1, NT // 2 - 1) as t:
                tile_steps(t, 0, False, False)
                tile_steps(t, 1, False, False)
            tile_steps(NT // 2 - 1, 0, False, False)
            tile_steps(NT // 2 - 1, 1, False, True)
            sums_out(NT - 1, 0)
            sums_out(NT - 1, 1)

            seq = sem("dve_seq")
            SEQ = 62

            class Chain:
                def __init__(self, c):
                    self.c, self.n = c, 0

                def add(self, ins):
                    self.n += 1
                    ins.then_inc(seq, 1)

                def wait(self):
                    dve.wait_ge(seq, self.c * SEQ + self.n)

                def __call__(self, ins):
                    self.add(ins)
                    self.wait()

            def rsqrt_c(step, v, y, w, mul, add):
                step(nc.vector.tensor_scalar(v, v, mul, add, ALU.mult, ALU.add))
                step(nc.vector.tensor_scalar(y.bitcast(I32), v.bitcast(I32), 1, None, ALU.logical_shift_right))
                step(nc.vector.tensor_scalar(y.bitcast(I32), y.bitcast(I32), -1.0, RSQRT_MAGIC, ALU.mult, ALU.add))
                for _ in range(3):
                    step(nc.vector.tensor_tensor(w, y, y, ALU.mult))
                    step(nc.vector.tensor_tensor(w, w, v, ALU.mult))
                    step(nc.vector.tensor_scalar(w, w, -0.5, 1.5, ALU.mult, ALU.add))
                    step(nc.vector.tensor_tensor(y, y, w, ALU.mult))

            def post_inv(c, ch):
                if isinstance(c, int) and c == 0:
                    dve.wait_ge(o_out_a, 2 * NT)
                    dve.wait_ge(o_out_v, 2 * NT)
                else:
                    dve.wait_ge(post_p, 4 * c)
                os_c = os_all[:, bass.ts(c, TC), :].rearrange("p i (n v) -> p (i n) v", v=9)
                ch(nc.vector.reciprocal(linv[:, :, :].rearrange("p n h -> p (n h)").unsqueeze(2), os_c[:, :, 8:9]))
                lv = linv[:, :, 1].rearrange("p (i n) -> p i n", i=TC)
                lm = lam[:, :, :].rearrange("p b n -> p (b n)").unsqueeze(1).to_broadcast([P, TC, 16])
                nc.vector.tensor_tensor(lv, lv, lm, ALU.mult).then_inc(post_v, 1)

            def post_rms(c, ch):
                dve.wait_ge(post_p, 4 * c + 3)
                ch(nc.vector.tensor_reduce(v_b[:, :], osq[:, :, :], AX.X, ALU.add))
                rsqrt_c(ch, v_b[:, :], v_a[:, :], v_c[:, :], 1.0 / DH, EPS)
                nc.vector.tensor_copy(v_c[:, :], v_a[:, :]).then_inc(post_v, 1)

            def post_res(c, ch):
                dve.wait_ge(post_e, 5 * c + 2)
                for b in range(2):
                    r = slice(64 * b, 64 * b + 64)
                    xr = x_all[r, bass.ts(c, TC), :].rearrange("p i d -> p (i d)")
                    ch(nc.vector.tensor_tensor(xr, xr, w_ps[b][r, :], ALU.add))
                for ii in range(TC):
                    i = c * TC + ii
                    if ii == 0:
                        dve.nop(nofuse=True)
                    ch.add(nc.vector.bn_stats(fstats[:, ii, :], x_all[:, bass.ds(i, 1), :].rearrange("p i d -> p (i d)")))
                ch.wait()
                nc.vector.tensor_copy(f_c[:, :], fstats[:, :, 1]).then_inc(post_v, 1)

            def post_norm(c, ch):
                st, mn, var, tmp = fstats, fmean[:, :], f_a[:, :], f_b[:, :]
                ch(nc.vector.tensor_tensor(mn, st[:, :, 1], st[:, :, 4], ALU.add))
                ch(nc.vector.tensor_tensor(tmp, st[:, :, 1], st[:, :, 4], ALU.subtract))
                ch(nc.vector.tensor_tensor(tmp, tmp, tmp, ALU.mult))
                ch(nc.vector.tensor_tensor(var, st[:, :, 2], st[:, :, 5], ALU.add))
                ch(nc.vector.scalar_tensor_tensor(out=var, in0=tmp, scalar=float(D) / 4, in1=var,
                                                  op0=ALU.mult, op1=ALU.add))
                ch(nc.vector.tensor_scalar(mn, mn, 0.5, None, ALU.mult))
                rsqrt_c(ch, var, f_b[:, :], f_c[:, :], 1.0 / D, EPS)
                if not isinstance(c, int) or c:
                    dve.wait_ge(post_e, 5 * c - 2)
                for ii in range(TC):
                    i = c * TC + ii
                    ins = nc.vector.tensor_scalar(fn[:, ii, :], x_all[:, bass.ds(i, 1), :].rearrange("p i d -> p (i d)"),
                                                  fmean[:, ii:ii + 1], f_b[:, ii:ii + 1], ALU.subtract, ALU.mult)
                    if ii < TC - 1:
                        ch(ins)
                ins.then_inc(post_v, 1)

            def post_sig(c, ch):
                dve.wait_ge(post_a, 5 * c + 4)
                ch(nc.vector.tensor_scalar(eneg[:, :, :], eneg[:, :, :], 1.0, None, ALU.add))
                ch(nc.vector.reciprocal(eneg[:, :, :], eneg[:, :, :]))
                dve.nop(nofuse=True)
                for ii in range(TC):
                    ch.add(nc.vector.max(top8[:, ii, :], logit[:, ii, :]))
                ch.wait()
                nc.vector.memset(top8[:, :, TOPK:8], NOMATCH).then_inc(post_v, 1)

            def post_gate(c, ch):
                dve.wait_ge(post_v, 6 * c + 5)
                dve.nop(nofuse=True)
                for ii in range(TC):
                    ch.add(nc.vector.match_replace(rest[:, ii, :], top8[:, ii, :], logit[:, ii, :], HIDE))
                ch.wait()
                ch(nc.vector.tensor_tensor(gate[:, :, :], rest[:, :, :], logit[:, :, :], ALU.not_equal))
                ch(nc.vector.tensor_tensor(gate[:, :, :], gate[:, :, :], eneg[:, :, :], ALU.mult))
                if not isinstance(c, int) or c:
                    dve.wait_ge(post_e, 5 * c)
                ch(nc.vector.tensor_copy(gpart[:, :, 0, :], gate[:, :, :]))
                ch(nc.vector.tensor_tensor(gate[:, :, :], gate[:, :, :], gpart[:, :, 0, :], ALU.subtract))
                ch(nc.vector.tensor_copy(gpart[:, :, 1, :], gate[:, :, :]))
                nc.vector.tensor_tensor(gpart[:, :, 2, :], gate[:, :, :], gpart[:, :, 1, :], ALU.subtract).then_inc(post_v, 1)

            def apply_gate(c, f, first):
                n = FT * c + f
                dve.wait_ge(relu_done, n + 1)
                dve.wait_ge(g_done, n + 1)
                if not first:
                    dve.wait_ge(used, n - 1)
                nc.vector.tensor_tensor(ghid[f % 2][:, :], g_ps[f % 2][:, :], hid[f % 2][:, :], ALU.mult).then_inc(gated, 1)

            def final_add(c, r):
                dve.wait_ge(y_turned, c + 1)
                xr = x_all[:, bass.ts(c, TC), :].rearrange("p i d -> p (i d)")
                nc.vector.tensor_tensor(y_sb[r][:, :, :].rearrange("p i d -> p (i d)"), xr, w_ps[0][:, :],
                                        ALU.add).then_inc(y_sum, 1)

            def chunk(c, r, first, last, stores):
                ch = Chain(c + 1)
                for f in range(FT):
                    apply_gate(c, f, first and f < 2)
                    if f == 3 and not first:
                        if stores is not None:
                            dve.wait_ge(stored[1 - r], stores)
                        final_add(c - 1, 1 - r)
                    if not last:
                        if f == 0:
                            post_inv(c + 1, ch)
                        if f == 4:
                            post_rms(c + 1, ch)
                        if f == 8:
                            post_res(c + 1, ch)
                            post_norm(c + 1, ch)
                        if f == 12:
                            post_sig(c + 1, ch)
                            post_gate(c + 1, ch)
                assert last or ch.n <= SEQ, ch.n
                while not last and ch.n < SEQ:
                    ch(nc.vector.memset(v_c[:, 0:1], 0.0))

            ch = Chain(0)
            post_inv(0, ch)
            post_rms(0, ch)
            post_res(0, ch)
            post_norm(0, ch)
            post_sig(0, ch)
            post_gate(0, ch)
            assert ch.n <= SEQ, ch.n
            while ch.n < SEQ:
                ch(nc.vector.memset(v_c[:, 0:1], 0.0))
            chunk(0, 0, True, False, None)
            chunk(1, 1, False, False, None)
            chunk(2, 0, False, False, None)
            with dve.Fori(1, (NC - 2) // 2) as u:
                chunk(2 * u + 1, 1, False, False, 16 * u)
                chunk(2 * u + 2, 0, False, False, 16 * u)
            chunk(NC - 1, 1, False, True, 16 * (NC // 2 - 1))
            dve.wait_ge(stored[1], 16 * (NC // 2 - 1))
            final_add(NC - 1, 1)


_INS = ['x', 'ctx_1024', 'mask_Bx16xSxS2_ff0', 'L0_xattn_W_q', 'L0_xattn_W_k', 'L0_xattn_W_v', 'L0_xattn_W_o',
        'L0_xattn_lambda_q1', 'L0_xattn_lambda_k1', 'L0_xattn_lambda_q2', 'L0_xattn_lambda_k2',
        'L0_xattn_rms_scale', 'L0_ffn_expert_sel', 'L0_ffn_keys', 'L0_ffn_values']
_OUTS = [((B, S, D), 'float32')]


def kernel(**inputs):
    import numpy as _np
    import concourse.bacc as _bacc
    from concourse import mybir as _mybir
    from concourse.bass_utils import run_bass_kernel_spmd as _run

    nc = _bacc.Bacc("TRN2", target_bir_lowering=False, num_devices=1)
    arrays, args = {}, []
    for name in _INS:
        a = _np.ascontiguousarray(inputs[name])
        arrays[f"in_{name}_dram"] = a
        args.append(nc.dram_tensor(f"in_{name}_dram", a.shape, _mybir.dt.from_np(a.dtype), kind="ExternalInput").ap())
    for i, (shape, dtype) in enumerate(_OUTS):
        dt = _mybir.dt.from_np(_np.dtype(dtype))
        args.append(nc.dram_tensor(f"out_{i}_dram", shape, dt, kind="ExternalOutput").ap())
    xattn_ffn(nc, *args)
    r = _run(nc, [arrays], core_ids=[0])
    return r.results[0]["out_0_dram"]
```

```python
from contextlib import ExitStack

import concourse.bass as bass
from concourse import mybir

ALU = mybir.AluOpType
ACT = mybir.ActivationFunctionType
AX = mybir.AxisListType
F32 = mybir.dt.float32
F16 = mybir.dt.float16
BF16 = mybir.dt.bfloat16
I32 = mybir.dt.int32

P = 128
B, S, D = 64, 64, 128
H, DH = 16, 8
E, F, TOPK = 32, 64, 4
LAMBDA_INIT = 0.8
EPS = 1e-5
QK_SCALE = DH ** -0.5
NT = B * S // P
NG = 4
NU = NT * NG
HP = H // 2
NC = 8
TC = NT // NC
CW = TC * P
FT = E * F // P
EPT = P // F
OW = 2 * HP * 2 * 9
RSQRT_MAGIC = float(0x5F3759DF)
HIDE = -3.0e38
NOMATCH = 3.0e38

SHIFT_LAG = 2
LOW_LAG = 3
TURN_LAG = 5
PV_LAG = 6
OUT_LAG = 7


def some(v):
    return not isinstance(v, int) or v > 0


def unit(i, e, g, lag):
    back, g2 = divmod(g - lag, NG)
    return i + back, (e + back) % 2, g2


def real(i):
    return not isinstance(i, int) or 0 <= i < NT


def xattn_ffn(nc, x, ctx_in, mask, W_q, W_k, W_v, W_o, lq1, lk1, lq2, lk2, rms_scale,
              expert_sel, keys, values, out):
    with ExitStack() as stack:
        def sb(name, shape, dt=F32):
            return stack.enter_context(nc.sbuf_tensor(name, shape, dt))

        def sem(name):
            return stack.enter_context(nc.semaphore(name))

        ident = sb("ident", [P, P])
        ident_h = sb("ident_h", [P, P], F16)
        ident_bf = sb("ident_bf", [P, P], BF16)
        head_cols = sb("head_cols", [P, NG])
        spread = sb("spread", [96, E * F], BF16)
        wq_raw = sb("wq_raw", [P, 2 * P])
        wk_raw = sb("wk_raw", [P, 2 * P])
        wq = sb("wq", [P, 2, P])
        wk = sb("wk", [P, 2, P])
        wv = sb("wv", [P, P])
        wo_raw = sb("wo_raw", [P, 2, D])
        wo = sb("wo", [P, 2, D])
        rms_col = sb("rms_col", [P, 1])
        rms_scaled = sb("rms_scaled", [P, 1])
        sel_rows = sb("sel_rows", [E, D])
        sel_hi = sb("sel_hi", [P, E], F16)
        sel_lo = sb("sel_lo", [P, E], F16)
        keys_sb = sb("keys_sb", [P, E * F])
        values_sb = sb("values_sb", [P, FT * D])
        keys_hi = sb("keys_hi", [P, E * F], F16)
        keys_lo = sb("keys_lo", [P, E * F], F16)
        values_hi = sb("values_hi", [P, FT * D], F16)
        values_lo = sb("values_lo", [P, FT * D], F16)
        lam_in = sb("lam_in", [P, 4, H * DH])
        lam_prod = sb("lam_prod", [P, 2, H * DH])
        lam_sum = sb("lam_sum", [P, 2, H])
        lam_exp = sb("lam_exp", [P, 2, H])
        lam_all = sb("lam_all", [P, H])
        lam = sb("lam", [P, 2, HP])

        x_all = sb("x_all", [P, NT, D])
        os_all = sb("os_all", [P, NT, OW])
        stats = sb("stats", [P, NT, 6])
        var = sb("var", [P, NT])
        tmp = sb("tmp", [P, NT])
        mean = sb("mean", [P, NT])
        rstd = sb("rstd", [P, NT])

        mask_sb = [sb(f"mask_sb{e}", [P, NG, 2, 2, S]) for e in range(2)]
        ctx_sb = [sb(f"ctx_sb{e}", [P, D]) for e in range(2)]
        xn = [sb(f"xn{e}", [P, D]) for e in range(2)]
        xc_t = [sb(f"xc_t{e}", [P, 2, P]) for e in range(2)]
        q_hi = [sb(f"q_hi{e}", [P, 2 * P], F16) for e in range(2)]
        q_lo = [sb(f"q_lo{e}", [P, 2 * P], F16) for e in range(2)]
        k_hi = [sb(f"k_hi{e}", [P, 2, P], F16) for e in range(2)]
        k_lo = [sb(f"k_lo{e}", [P, 2, P], F16) for e in range(2)]
        qm_hi = [sb(f"qm_hi{e}", [P, 4, NG, S], F16) for e in range(2)]
        qm_lo = [sb(f"qm_lo{e}", [P, 4, NG, S], F16) for e in range(2)]
        v_hi = [sb(f"v_hi{e}", [P, HP, 2, 2, 9], F16) for e in range(2)]
        v_lo = [sb(f"v_lo{e}", [P, HP, 2, 2, 9], F16) for e in range(2)]
        prob = [sb(f"prob{r}", [P, 4, 2, S]) for r in range(8)]
        rowmax = [sb(f"rowmax{r}", [P, 8]) for r in range(4)]
        p_hi = [sb(f"p_hi{r}", [P, 4, P], F16) for r in range(4)]
        p_lo = [sb(f"p_lo{r}", [P, 4, P], F16) for r in range(4)]
        p_t = [sb(f"p_t{r}", [P, 2, 4, P], F16) for r in range(2)]

        linv = sb("linv", [P, 64, 2])
        om = sb("om", [P, 64, 2, 8])
        oc = sb("oc", [P, 64, 8])
        osq = sb("osq", [P, 64, 8])
        on = sb("on", [P, 64, 8])
        sq_v = sb("sq_v", [P, 64 + TC])
        sq_y = sb("sq_y", [P, 64 + TC])
        sq_w = sb("sq_w", [P, 64 + TC])
        o_t = sb("o_t", [P, CW])
        fstats = sb("fstats", [P, TC, 6])
        fmean = sb("fmean", [P, TC])
        fvar = sb("fvar", [P, TC])
        ftmp = sb("ftmp", [P, TC])
        fn = sb("fn", [P, TC, D])
        fn_hi = [sb(f"fn_hi{r}", [P, CW], F16) for r in range(2)]
        fn_lo = [sb(f"fn_lo{r}", [P, CW], F16) for r in range(2)]
        logit = sb("logit", [P, TC, E])
        sig = sb("sig", [P, TC, E])
        top8 = sb("top8", [P, TC, 8])
        rest = sb("rest", [P, TC, E])
        gate = sb("gate", [P, TC, E])
        gpart = sb("gpart", [P, TC, 3, E], BF16)
        gate_t = [sb(f"gate_t{r}", [96, CW], BF16) for r in range(2)]
        hid = [sb(f"hid{r}", [P, CW]) for r in range(2)]
        ghid = [sb(f"ghid{r}", [P, CW]) for r in range(4)]
        gh_hi = [sb(f"gh_hi{r}", [P, CW], F16) for r in range(4)]
        gh_lo = [sb(f"gh_lo{r}", [P, CW], F16) for r in range(4)]
        y_t = sb("y_t", [P, CW])
        y_sb = [sb(f"y_sb{r}", [P, TC, D]) for r in range(2)]

        bank = [stack.enter_context(nc.psum_tensor(f"bank{r}", [P, 512], F32)) for r in range(8)]
        sc_ps, pt_ps, o_ps, m_ps, m2_ps = bank[0:2], bank[2:4], bank[4:6], bank[6], bank[7]
        w_ps, h_ps, g_ps, y_ps, t_ps = bank[0:2], bank[2:4], bank[4:6], bank[6], bank[7]

        x_in = [sem("x_in0"), sem("x_in1")]
        w_in = sem("w_in")
        lam_in_s = sem("lam_in_s")
        wp_in = sem("wp_in")
        mask_in = [sem(f"mask_in{e}") for e in range(2)]
        ctx_in_s = [sem(f"ctx_in{e}") for e in range(2)]
        ident0 = sem("ident0")
        ident_ok = sem("ident_ok")
        dve_own = sem("dve_own")
        heads_ok = sem("heads_ok")
        consts_ok = sem("consts_ok")
        w_perm = sem("w_perm")
        rms_ok = sem("rms_ok")
        wo_ok = sem("wo_ok")
        sel_turned = sem("sel_turned")
        sel_hi_ok = sem("sel_hi_ok")
        sel_lo_ok = sem("sel_lo_ok")
        w_hi_ok = sem("w_hi_ok")
        w_lo_ok = sem("w_lo_ok")
        lam_sums = sem("lam_sums")
        lam_exps = sem("lam_exps")
        v_init = sem("v_init")
        xn_ready = sem("xn_ready")
        tr_done = sem("tr_done")
        xt_ready = sem("xt_ready")
        qk_done = sem("qk_done")
        vp_done = sem("vp_done")
        qk_hi = sem("qk_hi")
        qk_lo = sem("qk_lo")
        v_hi_out = sem("v_hi_out")
        v_lo_out = sem("v_lo_out")
        qm_ready = sem("qm_ready")
        scored = sem("scored")
        masked = sem("masked")
        maxed = sem("maxed")
        shifted = sem("shifted")
        exped = sem("exped")
        high = sem("high")
        low = sem("low")
        turned = sem("turned")
        turned_out = sem("turned_out")
        pv_done = sem("pv_done")
        o_out_a = sem("o_out_a")
        o_out_v = sem("o_out_v")
        inv_done = sem("inv_done")
        pool_own = sem("pool_own")
        sq_done = sem("sq_done")
        rr_done = sem("rr_done")
        on_done = sem("on_done")
        otr_done = sem("otr_done")
        ot_out = sem("ot_out")
        wo_done = sem("wo_done")
        res_done = sem("res_done")
        fn_done = sem("fn_done")
        ftr_done = sem("ftr_done")
        fnh_out = sem("fnh_out")
        fnl_out = sem("fnl_out")
        lg_done = sem("lg_done")
        lg_out = sem("lg_out")
        parts_done = sem("parts_done")
        gtr_done = sem("gtr_done")
        gt_out = sem("gt_out")
        y_out = sem("y_out")
        y_turned = sem("y_turned")
        y_sum = sem("y_sum")
        stored = [sem(f"stored{r}") for r in range(2)]
        dve_seq = sem("dve_seq")
        h_done = sem("h_done")
        g_done = sem("g_done")
        relu_done = sem("relu_done")
        gated = sem("gated")
        gh_high = sem("gh_high")
        gh_low = sem("gh_low")
        used = sem("used")

        x_v = x.rearrange("b s d -> (b s) d").rearrange("(i p) d -> p i d", p=P)
        out_v = out.rearrange("b s d -> (b s) d").rearrange("(i p) d -> p i d", p=P)
        ctx_v = ctx_in.rearrange("b s d -> (b s) d").rearrange("(i p) d -> p i d", p=P)
        mask_v = mask.rearrange("b (n j) q k -> (j q) b n k", j=2)

        X0 = 4
        N_W = 16 * 3
        N_LAM = 16 * 4
        N_WP = 16 * (2 * HP + 16 + 3)

        block = stack.enter_context(nc.Block())

        @block.sync
        def _(sp):
            def load_mask(i, e):
                for b in range(2):
                    sp.dma_start(mask_sb[e][:, :, :, b, :].rearrange("p g r k -> p (g r) k"),
                                 mask_v[:, 2 * i + b]).then_inc(mask_in[e], 16)

            def load_ctx(i, e):
                sp.dma_start(ctx_sb[e][:, :], ctx_v[:, i, :]).then_inc(ctx_in_s[e], 16)

            sp.dma_start(x_all[:, 0:X0, :], x_v[:, 0:X0, :]).then_inc(x_in[0], 16)
            load_ctx(0, 0)
            sp.dma_start(wq_raw[:, :], W_q).then_inc(w_in, 16)
            sp.dma_start(wk_raw[:, :], W_k).then_inc(w_in, 16)
            sp.dma_start(wv[:, :], W_v).then_inc(w_in, 16)
            load_ctx(1, 1)
            load_mask(0, 0)
            sp.dma_start(x_all[:, X0:NT, :], x_v[:, X0:NT, :]).then_inc(x_in[1], 16)
            load_mask(1, 1)
            for a in range(4):
                src = (lq1, lk1, lq2, lk2)[a].rearrange("(o h) d -> o (h d)", o=1)
                sp.dma_start(lam_in[:, a, :], src.to_broadcast([P, H * DH])).then_inc(lam_in_s, 16)

            def reload(i, e):
                sp.wait_ge(tr_done, i - 1)
                load_ctx(i, e)
                sp.wait_ge(masked, NG * (i - 1))
                load_mask(i, e)

            reload(2, 0)
            reload(3, 1)
            sp.dma_start(keys_sb[:, :].rearrange("d (e f) -> d e f", e=E),
                         keys.rearrange("e d f -> d e f")).then_inc(wp_in, 16)
            sp.dma_start(values_sb[:, :].rearrange("p (t d) -> p t d", t=FT),
                         values.rearrange("(t e) f d -> (e f) t d", e=EPT)).then_inc(wp_in, 16)
            sp.dma_start(sel_rows[:, :], expert_sel).then_inc(wp_in, 16)
            reload(4, 0)
            for b in range(2):
                for hp in range(HP):
                    r0 = (HP * b + hp) * DH
                    src = W_o.rearrange("(hp j d) n -> hp d j n", j=2, d=DH)[hp]
                    sp.dma_start(wo_raw[r0:r0 + DH, :, :], src).then_inc(wp_in, 16)
            reload(5, 1)
            for r in range(16):
                sp.dma_start(rms_col[DH * r:DH * r + DH, :],
                             rms_scale.rearrange("(d o) -> d o", o=1)).then_inc(wp_in, 16)
            with sp.Fori(3, NT // 2) as t:
                reload(2 * t, 0)
                reload(2 * t + 1, 1)

        @block.gpsimd
        def _(pool):
            nc.gpsimd.memset(ident[:, :], 0.0).then_inc(ident0, 1)
            pool.wait_ge(ident0, 1)
            nc.gpsimd.affine_select(out=ident[:, :], in_=ident[:, :], compare_op=ALU.not_equal, fill=1.0,
                                    base=0, pattern=[[-1, P]], channel_multiplier=1).then_inc(ident_ok, 1)
            pool.wait_ge(heads_ok, 1)

            def one_head(i, e, part):
                if not real(i):
                    return
                q, qm = ((q_hi, qm_hi), (q_lo, qm_lo))[part]
                pool.wait_ge((qk_hi, qk_lo)[part], 2 * i + 1)
                if some(i - 1):
                    pool.wait_ge(scored, NG * (i - 1))
                kept = head_cols[:, :].unsqueeze(1).unsqueeze(3).to_broadcast([P, 4, NG, S])
                src = q[e][:, :].rearrange("p (n s) -> p n s", n=4).unsqueeze(2).to_broadcast([P, 4, NG, S])
                nc.gpsimd.tensor_tensor(qm[e][:, :, :, :], src, kept, ALU.mult).then_inc(qm_ready, 1)

            def low_part(i, e, g):
                if not real(i):
                    return
                n = NG * i + g
                pool.wait_ge(high, n + 1)
                if some(n - 3):
                    pool.wait_ge(turned, n - 3)
                nc.gpsimd.tensor_tensor(p_lo[g][:, :, :].rearrange("p a k -> p (a k)"),
                                        prob[4 * e + g][:, :, :, :].rearrange("p a b k -> p (a b k)"),
                                        p_hi[g][:, :, :].rearrange("p a k -> p (a k)"),
                                        ALU.subtract).then_inc(low, 1)

            def tile_steps(i, e):
                for g in range(NG):
                    low_part(*unit(i, e, g, LOW_LAG))
                    if g == 1:
                        one_head(i + 1, 1 - e, 0)
                    if g == 2:
                        one_head(i + 1, 1 - e, 1)

            one_head(0, 0, 0)
            one_head(0, 0, 1)
            for i in range(4):
                tile_steps(i, i % 2)
            pool.wait_ge(w_hi_ok, 2)
            nc.gpsimd.tensor_tensor(keys_lo[:, :], keys_sb[:, :], keys_hi[:, :], ALU.subtract).then_inc(w_lo_ok, 1)
            nc.gpsimd.tensor_tensor(values_lo[:, :], values_sb[:, :], values_hi[:, :], ALU.subtract).then_inc(w_lo_ok, 1)
            with pool.Fori(2, NT // 2 - 1) as t:
                tile_steps(2 * t, 0)
                tile_steps(2 * t + 1, 1)
            for i in range(NT - 2, NT + 2):
                tile_steps(i, i % 2)

            def heads(c):
                pool.wait_ge(inv_done, c + 1)
                if some(c):
                    pool.wait_ge(on_done, c)
                os_c = os_all[:, bass.ts(c, TC), :].rearrange("p i (n v) -> p (i n) v", v=9)
                nc.gpsimd.tensor_tensor(om[:, :, :, :].rearrange("p n h v -> p (n h) v"), os_c[:, :, 0:8],
                                        linv[:, :, :].rearrange("p n h -> p (n h)").unsqueeze(2).to_broadcast([P, P, 8]),
                                        ALU.mult).then_inc(pool_own, 1)
                pool.wait_ge(pool_own, 2 * c + 1)
                nc.gpsimd.tensor_tensor(oc[:, :, :], om[:, :, 0, :], om[:, :, 1, :], ALU.subtract).then_inc(pool_own, 1)
                pool.wait_ge(pool_own, 2 * c + 2)
                nc.gpsimd.tensor_tensor(osq[:, :, :], oc[:, :, :], oc[:, :, :], ALU.mult).then_inc(sq_done, 1)

            def scale_heads(c):
                pool.wait_ge(rr_done, c + 1)
                if some(c):
                    pool.wait_ge(otr_done, c)
                nc.gpsimd.tensor_tensor(on[:, :, :], oc[:, :, :],
                                        sq_y[:, 0:64].unsqueeze(2).to_broadcast([P, 64, 8]),
                                        ALU.mult).then_inc(on_done, 1)

            def low_hidden(c, f):
                n = FT * c + f
                pool.wait_ge(gh_high, n + 1)
                if some(n - 3):
                    pool.wait_ge(used, n - 3)
                nc.gpsimd.tensor_tensor(gh_lo[f % 4][:, :], ghid[f % 4][:, :], gh_hi[f % 4][:, :],
                                        ALU.subtract).then_inc(gh_low, 1)

            def chunk(c, part1):
                for f in range(FT):
                    if part1 and f == 1:
                        heads(c + 2)
                    if part1 and f == 7:
                        scale_heads(c + 2)
                    low_hidden(c, f)

            heads(0)
            scale_heads(0)
            heads(1)
            scale_heads(1)
            chunk(0, True)
            chunk(1, True)
            with pool.Fori(1, NC // 2 - 1) as u:
                chunk(2 * u, True)
                chunk(2 * u + 1, True)
            chunk(NC - 2, False)
            chunk(NC - 1, False)

        @block.tensor
        def _(pe):
            def pre_turn(i, e, nth):
                if not real(i):
                    return
                pe.wait_ge(xn_ready, i + 1)
                pe.wait_ge(ctx_in_s[e], 16 * nth)
                if some(i - 2):
                    pe.wait_ge(v_lo_out, 2 * (i - 2))
                if some(i):
                    pe.wait_ge(xt_ready, i)
                pe.transpose(m_ps[:, 0:P], xn[e][:, :], ident[:, :])
                pe.transpose(m_ps[:, P:2 * P], ctx_sb[e][:, :], ident[:, :]).then_inc(tr_done, 1)

            def project_qk(i, e):
                if not real(i):
                    return
                pe.wait_ge(xt_ready, i + 1)
                if some(i):
                    pe.wait_ge(qk_lo, 2 * i)
                for h in range(2):
                    pe.matmul(m2_ps[:, h * P:(h + 1) * P], wq[:, h, :], xc_t[e][:, 0, :], start=(h == 0), stop=True,
                              skip_group_check=True)
                for h in range(2):
                    mm = pe.matmul(m2_ps[:, (2 + h) * P:(3 + h) * P], wk[:, h, :], xc_t[e][:, 1, :],
                                   start=False, stop=True, skip_group_check=True)
                mm.then_inc(qk_done, 1)

            def project_v(i, e):
                if not real(i):
                    return
                if some(i):
                    pe.wait_ge(v_lo_out, 2 * i)
                if some(i + 1) and real(i + 1):
                    pe.wait_ge(xt_ready, i + 2)
                pe.matmul(m_ps[:, 2 * P:3 * P], xc_t[e][:, 1, :], wv[:, :], start=True,
                          stop=True, skip_group_check=True).then_inc(vp_done, 1)

            def scores(i, e, g):
                if not real(i):
                    return
                n = NG * i + g
                if g == 0:
                    pe.wait_ge(qm_ready, 2 * i + 2)
                    pe.wait_ge(qk_lo, 2 * i + 2)
                if some(n - 1):
                    pe.wait_ge(masked, n - 1)
                rows = slice(32 * g, 32 * g + 32)
                for p in range(2):
                    for h in range(2):
                        for b in range(2):
                            o = ((p * 2 + h) * 2 + b) * S
                            for a, (ql, kl) in enumerate(((qm_hi, k_hi), (qm_hi, k_lo), (qm_lo, k_hi))):
                                mm = pe.matmul(sc_ps[g % 2][:, o:o + S],
                                               ql[e][rows, 2 * h + b, 2 * p:2 * p + 2, :].rearrange("p j s -> p (j s)"),
                                               kl[e][rows, h, b * S:b * S + S],
                                               start=(o == 0 and a == 0), stop=(a == 2), skip_group_check=True)
                mm.then_inc(scored, 1)

            def turn(i, e, g):
                if not real(i):
                    return
                n = NG * i + g
                pe.wait_ge(low, n + 1)
                if some(n - 1):
                    pe.wait_ge(turned_out, n - 1)
                pt = pt_ps[g % 2][:, :].bitcast(F16)
                for part, src in enumerate((p_hi, p_lo)):
                    for a in range(4):
                        o = (4 * part + a) * P
                        mm = pe.transpose(pt[:, o:o + P], src[g][:, a, :], ident_h[:, :])
                mm.then_inc(turned, 1)

            def attend(i, e, g):
                if not real(i):
                    return
                n = NG * i + g
                pe.wait_ge(turned_out, n + 1)
                if g == 0:
                    pe.wait_ge(v_lo_out, 2 * i + 2)
                pair = 2 * i + g // 2
                if g % 2 == 0 and some(pair - 1):
                    pe.wait_ge(o_out_a, pair - 1)
                    pe.wait_ge(o_out_v, pair - 1)
                for p in range(2):
                    for h in range(2):
                        o = (((g % 2) * 2 + p) * 2 + h) * 36
                        for a, (part, v) in enumerate(((0, v_hi), (0, v_lo), (1, v_hi))):
                            mm = pe.matmul(o_ps[g // 2][:, o:o + 36], p_t[g % 2][:, part, 2 * p + h, :],
                                           v[e][:, 2 * g + p, :, :, :].rearrange("p j b v -> p (j b v)"),
                                           start=(g % 2 == 0 and o == 0 and a == 0), stop=(a == 2),
                                           skip_group_check=True)
                mm.then_inc(pv_done, 1)

            def tile_steps(t, e):
                i = 2 * t + e
                for g in range(NG):
                    scores(i, e, g)
                    turn(*unit(i, e, g, TURN_LAG))
                    if g == 2:
                        project_v(i, e)
                        pre_turn(i + 2, e, t + 2)
                    if g == 3:
                        project_qk(i + 2, e)
                    attend(*unit(i, e, g, PV_LAG))

            pe.wait_ge(ident_ok, 1)
            pre_turn(0, 0, 1)
            pe.wait_ge(w_in, N_W)
            pe.wait_ge(w_perm, 4)
            project_qk(0, 0)
            pre_turn(1, 1, 1)
            project_qk(1, 1)
            pe.wait_ge(consts_ok, 2)
            for t in range(2):
                tile_steps(t, 0)
                tile_steps(t, 1)
            with pe.Fori(2, NT // 2 - 1) as t:
                tile_steps(t, 0)
                tile_steps(t, 1)
            for t in range(NT // 2 - 1, NT // 2 + 1):
                tile_steps(t, 0)
                tile_steps(t, 1)

            pe.wait_ge(wp_in, N_WP)
            pe.wait_ge(qk_lo, 2 * NT)
            pe.transpose(t_ps[:, 0:E], sel_rows[:, :], ident[0:E, 0:E]).then_inc(sel_turned, 1)
            pe.wait_ge(sel_hi_ok, 1)
            pe.wait_ge(sel_lo_ok, 1)
            pe.wait_ge(wo_ok, 1)
            pe.wait_ge(w_lo_ok, 2)
            pe.wait_ge(consts_ok, 5)

            def turn_heads(c):
                pe.wait_ge(on_done, c + 1)
                if some(c):
                    pe.wait_ge(lg_out, 2 * c)
                for ii in range(TC):
                    mm = pe.transpose(t_ps[:, ii * P:(ii + 1) * P],
                                      on[:, 16 * ii:16 * ii + 16, :].rearrange("p n v -> p (n v)"), ident[:, :])
                mm.then_inc(otr_done, 1)

            def project_out(c):
                pe.wait_ge(ot_out, c + 1)
                if some(c - 2):
                    pe.wait_ge(y_sum, c - 2)
                pe.nop(nofuse=True)
                for b in range(2):
                    r = slice(64 * b, 64 * b + 64)
                    for ii in range(TC):
                        for j in range(2):
                            mm = pe.matmul(w_ps[b][r, ii * P:(ii + 1) * P],
                                           o_t[r, ii * P + 64 * j:ii * P + 64 * j + 64], wo[r, j, :],
                                           start=(j == 0 and ii == 0), stop=(j == 1), skip_group_check=True)
                mm.then_inc(wo_done, 1)

            def turn_norm(c):
                pe.wait_ge(fn_done, c + 1)
                if some(c):
                    pe.wait_ge(gt_out, c)
                for ii in range(TC):
                    mm = pe.transpose(t_ps[:, ii * P:(ii + 1) * P], fn[:, ii, :], ident[:, :])
                mm.then_inc(ftr_done, 1)

            def logits(c, r):
                pe.wait_ge(fnl_out, c + 1)
                for ii in range(TC):
                    for a, (xs, ws) in enumerate(((fn_hi, sel_hi), (fn_hi, sel_lo), (fn_lo, sel_hi))):
                        mm = pe.matmul(t_ps[:, ii * E:(ii + 1) * E], xs[r][:, ii * P:(ii + 1) * P], ws[:, :],
                                       start=(ii == 0 and a == 0), stop=(a == 2), skip_group_check=True)
                mm.then_inc(lg_done, 1)

            def turn_gates(c):
                pe.wait_ge(parts_done, c + 1)
                tb = t_ps[:, :].bitcast(BF16)
                for ii in range(TC):
                    mm = pe.transpose(tb[0:96, ii * P:(ii + 1) * P],
                                      gpart[:, ii, :, :].rearrange("p a e -> p (a e)"), ident_bf[:, :])
                mm.then_inc(gtr_done, 1)

            def hidden(c, r, f):
                n = FT * c + f
                if some(n - 1):
                    pe.wait_ge(relu_done, n - 1)
                for a, (ws, xs) in enumerate(((keys_hi, fn_hi), (keys_hi, fn_lo), (keys_lo, fn_hi))):
                    mm = pe.matmul(h_ps[f % 2][:, :], ws[:, f * P:(f + 1) * P], xs[r][:, :], start=(a == 0),
                                   stop=(a == 2))
                mm.then_inc(h_done, 1)
                if f == 0:
                    pe.wait_ge(gt_out, c + 1)
                if some(n - 1):
                    pe.wait_ge(gated, n - 1)
                pe.matmul(g_ps[f % 2][:, :], spread[:, f * P:(f + 1) * P], gate_t[r][:, :], start=True,
                          stop=True).then_inc(g_done, 1)

            def down(c, f):
                n = FT * c + f
                pe.wait_ge(gh_low, n + 1)
                if f == 0 and some(c):
                    pe.wait_ge(y_out, c)
                for a, (ws, xs) in enumerate(((values_hi, gh_hi), (values_hi, gh_lo), (values_lo, gh_hi))):
                    mm = pe.matmul(y_ps[:, :], ws[:, f * P:(f + 1) * P], xs[f % 4][:, :],
                                   start=(f == 0 and a == 0), stop=(f == FT - 1 and a == 2))
                mm.then_inc(used, 1)

            def turn_y(c):
                pe.wait_ge(y_out, c + 1)
                if c + 2 < NC if isinstance(c, int) else True:
                    pe.wait_ge(res_done, c + 3)
                for ii in range(TC):
                    mm = pe.transpose(w_ps[0][:, ii * P:(ii + 1) * P], y_t[:, ii * P:(ii + 1) * P], ident[:, :])
                mm.then_inc(y_turned, 1)

            def chunk(c, r, part1, part2):
                for f in range(FT + 3):
                    if f < FT:
                        hidden(c, r, f)
                    if f >= 3:
                        down(c, f - 3)
                    if f == 3 and some(c):
                        turn_y(c - 1)
                    if part2 and f == 8:
                        turn_norm(c + 1)
                    if part2 and f == 10:
                        logits(c + 1, 1 - r)
                    if part1 and f == 12:
                        turn_heads(c + 2)
                    if part1 and f == 13:
                        project_out(c + 2)
                    if part2 and f == 15:
                        turn_gates(c + 1)

            turn_heads(0)
            pe.wait_ge(masked, NU)
            project_out(0)
            turn_norm(0)
            logits(0, 0)
            turn_heads(1)
            project_out(1)
            turn_gates(0)
            pe.wait_ge(turned_out, NU)
            pe.wait_ge(o_out_a, NU // 2)
            pe.wait_ge(o_out_v, NU // 2)
            pe.wait_ge(v_lo_out, 2 * NT)
            chunk(0, 0, True, True)
            chunk(1, 1, True, True)
            with pe.Fori(1, NC // 2 - 1) as u:
                chunk(2 * u, 0, True, True)
                chunk(2 * u + 1, 1, True, True)
            chunk(NC - 2, 0, False, True)
            chunk(NC - 1, 1, False, False)
            turn_y(NC - 1)

        @block.scalar
        def _(act):
            act.wait_ge(w_in, N_W)
            for raw, w in ((wq_raw, wq), (wk_raw, wk)):
                for h in range(2):
                    src = raw[:, :].rearrange("p (n a d) -> p n a d", n=H, a=2)[:, :, h, :]
                    nc.scalar.copy(w[:, h, :].rearrange("p (n d) -> p n d", n=H), src).then_inc(w_perm, 1)

            def pre_turn_out(i, e):
                if not real(i):
                    return
                act.wait_ge(tr_done, i + 1)
                if some(i - 1):
                    act.wait_ge(qk_done, i - 1)
                    act.wait_ge(vp_done, i - 1)
                nc.scalar.copy(xc_t[e][:, :, :].rearrange("p a t -> p (a t)"), m_ps[:, 0:2 * P]).then_inc(xt_ready, 1)

            def qk_high(i, e):
                if not real(i):
                    return
                act.wait_ge(qk_done, i + 1)
                if some(i - 1):
                    act.wait_ge(qm_ready, 2 * (i - 1))
                    act.wait_ge(scored, NG * (i - 1))
                    act.wait_ge(qk_lo, 2 * (i - 1))
                nc.scalar.mul(q_hi[e][:, :], m2_ps[:, 0:2 * P], QK_SCALE).then_inc(qk_hi, 1)
                nc.scalar.copy(k_hi[e][:, :, :].rearrange("p h t -> p (h t)"), m2_ps[:, 2 * P:4 * P]).then_inc(qk_hi, 1)

            def v_high(i, e):
                if not real(i):
                    return
                act.wait_ge(vp_done, i + 1)
                if some(i - 1):
                    act.wait_ge(pv_done, NG * (i - 1))
                else:
                    act.wait_ge(v_init, 8)
                for b in range(2):
                    r = slice(64 * b, 64 * b + 64)
                    nc.scalar.copy(v_hi[e][r, :, :, b, 0:8].rearrange("p n j v -> p (n j) v"),
                                   m_ps[r, 2 * P:3 * P].rearrange("p (n v) -> p n v", v=DH)).then_inc(v_hi_out, 1)

            def exponent(i, e, g):
                if not real(i):
                    return
                act.wait_ge(shifted, NG * i + g + 1)
                pr = prob[4 * e + g][:, :, :, :].rearrange("p a b k -> p (a b k)")
                nc.scalar.activation(pr, pr, ACT.Exp).then_inc(exped, 1)

            def high_part(i, e, g):
                if not real(i):
                    return
                n = NG * i + g
                act.wait_ge(exped, n + 1)
                if some(n - 3):
                    act.wait_ge(turned, n - 3)
                    act.wait_ge(low, n - 3)
                nc.scalar.copy(p_hi[g][:, :, :].rearrange("p a k -> p (a k)"),
                               prob[4 * e + g][:, :, :, :].rearrange("p a b k -> p (a b k)")).then_inc(high, 1)

            def turn_out(i, e, g):
                if not real(i):
                    return
                n = NG * i + g
                act.wait_ge(turned, n + 1)
                if some(n - 1):
                    act.wait_ge(pv_done, n - 1)
                nc.scalar.copy(p_t[g % 2][:, :, :, :].rearrange("p a n k -> p (a n k)").bitcast(F32),
                               pt_ps[g % 2][:, :]).then_inc(turned_out, 1)

            def sums_out(i, e, g):
                if not real(i):
                    return
                m = g // 2
                act.wait_ge(pv_done, NG * i + g + 1)
                src = o_ps[m][0:64, 0:288].rearrange("p (n v) -> p n v", v=36)[:, :, 0:18]
                dst = os_all[0:64, bass.ds(i, 1), :].rearrange("p i (b n v) -> p (i n) b v", b=2, v=9)
                nc.scalar.copy(dst[:, 8 * m:8 * m + 8, :, :], src.rearrange("p n (b v) -> p n b v", b=2)).then_inc(o_out_a, 1)

            def tile_steps(i, e):
                for g in range(NG):
                    if g == 0:
                        qk_high(i + 1, 1 - e)
                    if g == 3:
                        pre_turn_out(i + 2, e)
                        v_high(i, e)
                    exponent(*unit(i, e, g, SHIFT_LAG))
                    turn_out(*unit(i, e, g, TURN_LAG))
                    high_part(*unit(i, e, g, SHIFT_LAG))
                    if g % 2 == 0:
                        sums_out(*unit(i, e, g, OUT_LAG))

            pre_turn_out(0, 0)
            qk_high(0, 0)
            pre_turn_out(1, 1)
            act.wait_ge(lam_sums, 1)
            nc.scalar.activation(lam_exp[:, :, :], lam_sum[:, :, :], ACT.Exp).then_inc(lam_exps, 1)
            for i in range(4):
                tile_steps(i, i % 2)
            act.wait_ge(wp_in, N_WP)
            nc.scalar.copy(keys_hi[:, :], keys_sb[:, :]).then_inc(w_hi_ok, 1)
            nc.scalar.copy(values_hi[:, :], values_sb[:, :]).then_inc(w_hi_ok, 1)
            nc.scalar.mul(rms_scaled[:, :], rms_col[:, :], 1.0 - LAMBDA_INIT).then_inc(rms_ok, 1)
            act.wait_ge(rms_ok, 1)
            nc.scalar.activation(wo[:, :, :], wo_raw[:, :, :], ACT.Copy, scale=rms_scaled[:, 0:1]).then_inc(wo_ok, 1)
            with act.Fori(2, NT // 2 - 1) as t:
                tile_steps(2 * t, 0)
                tile_steps(2 * t + 1, 1)
            for i in range(NT - 2, NT + 2):
                tile_steps(i, i % 2)

            act.wait_ge(sel_turned, 1)
            nc.scalar.copy(sel_hi[:, :], t_ps[:, 0:E]).then_inc(sel_hi_ok, 1)

            def heads_out(c):
                act.wait_ge(otr_done, c + 1)
                if some(c):
                    act.wait_ge(wo_done, c)
                nc.scalar.copy(o_t[:, :], t_ps[:, :]).then_inc(ot_out, 1)

            def norm_out(c, r):
                act.wait_ge(ftr_done, c + 1)
                if some(c - 1):
                    act.wait_ge(h_done, FT * (c - 1))
                nc.scalar.copy(fn_hi[r][:, :], t_ps[:, :]).then_inc(fnh_out, 1)

            def logits_out(c):
                act.wait_ge(lg_done, c + 1)
                if some(c):
                    act.wait_ge(parts_done, c)
                src = t_ps[:, 0:TC * E]
                nc.scalar.activation(sig[:, :, :].rearrange("p i e -> p (i e)"), src, ACT.Exp, scale=-1.0).then_inc(lg_out, 1)
                nc.scalar.copy(logit[:, :, :].rearrange("p i e -> p (i e)"), src).then_inc(lg_out, 1)

            def gates_out(c, r):
                act.wait_ge(gtr_done, c + 1)
                if some(c - 1):
                    act.wait_ge(g_done, FT * (c - 1))
                nc.scalar.copy(gate_t[r][:, :], t_ps[:, :].bitcast(BF16)[0:96, 0:CW]).then_inc(gt_out, 1)

            def relu(c, f):
                n = FT * c + f
                act.wait_ge(h_done, n + 1)
                if some(n - 1):
                    act.wait_ge(gated, n - 1)
                nc.scalar.activation(hid[f % 2][:, :], h_ps[f % 2][:, :], ACT.Relu).then_inc(relu_done, 1)

            def high_hidden(c, f):
                n = FT * c + f
                act.wait_ge(gated, n + 1)
                if some(n - 3):
                    act.wait_ge(used, n - 3)
                nc.scalar.copy(gh_hi[f % 4][:, :], ghid[f % 4][:, :]).then_inc(gh_high, 1)

            def y_copy(c):
                act.wait_ge(used, FT * c + FT)
                if some(c):
                    act.wait_ge(y_turned, c)
                nc.scalar.copy(y_t[:, :], y_ps[:, :]).then_inc(y_out, 1)

            def store(c, r):
                act.wait_ge(y_sum, c + 1)
                act.dma_start(out_v[:, bass.ts(c, TC), :], y_sb[r][:, :, :]).then_inc(stored[r], 16)

            def chunk(c, r, part1, part2):
                for f in range(FT + 1):
                    if f < FT:
                        relu(c, f)
                    if f >= 1:
                        high_hidden(c, f - 1)
                    if f == 2 and some(c):
                        y_copy(c - 1)
                    if f == 6 and some(c):
                        store(c - 1, 1 - r)
                    if part2 and f == 8:
                        norm_out(c + 1, 1 - r)
                    if part2 and f == 10:
                        logits_out(c + 1)
                    if part1 and f == 12:
                        heads_out(c + 2)
                    if part2 and f == 15:
                        gates_out(c + 1, 1 - r)

            heads_out(0)
            norm_out(0, 0)
            logits_out(0)
            heads_out(1)
            gates_out(0, 0)
            chunk(0, 0, True, True)
            chunk(1, 1, True, True)
            with act.Fori(1, NC // 2 - 1) as u:
                chunk(2 * u, 0, True, True)
                chunk(2 * u + 1, 1, True, True)
            chunk(NC - 2, 0, False, True)
            chunk(NC - 1, 1, False, False)
            y_copy(NC - 1)
            store(NC - 1, 1)
            for r in range(2):
                act.wait_ge(stored[r], 16 * (NC // 2))

        @block.vector
        def _(dve):
            own = [0]

            def step(ins):
                own[0] += 1
                ins.then_inc(dve_own, 1)
                dve.wait_ge(dve_own, own[0])

            dve.wait_ge(ident_ok, 1)
            nc.vector.tensor_reduce(head_cols[:, :], ident[:, :].rearrange("p (g j d) -> p j g d", g=NG, j=NG),
                                    AX.XY, ALU.add).then_inc(heads_ok, 1)
            nc.vector.tensor_copy(ident_h[:, :], ident[:, :]).then_inc(consts_ok, 1)

            def rsqrt(step, v, y, w, iterations=3):
                step(nc.vector.tensor_scalar(y.bitcast(I32), v.bitcast(I32), 1, None, ALU.logical_shift_right))
                step(nc.vector.tensor_scalar(y.bitcast(I32), y.bitcast(I32), -1.0, RSQRT_MAGIC, ALU.mult, ALU.add))
                for _ in range(iterations):
                    newton(step, v, y, w)

            def newton(step, v, y, w):
                step(nc.vector.tensor_tensor(w, y, y, ALU.mult))
                step(nc.vector.scalar_tensor_tensor(out=w, in0=w, scalar=-0.5, in1=v, op0=ALU.mult, op1=ALU.mult))
                step(nc.vector.scalar_tensor_tensor(out=y, in0=w, scalar=1.5, in1=y, op0=ALU.add, op1=ALU.mult))

            def moments(step, st, mn, vr, tm):
                step(nc.vector.tensor_tensor(mn, st[:, :, 1], st[:, :, 4], ALU.add))
                step(nc.vector.tensor_tensor(tm, st[:, :, 1], st[:, :, 4], ALU.subtract))
                step(nc.vector.tensor_tensor(tm, tm, tm, ALU.mult))
                step(nc.vector.tensor_tensor(vr, st[:, :, 2], st[:, :, 5], ALU.add))
                step(nc.vector.scalar_tensor_tensor(out=vr, in0=tm, scalar=float(D) / 4, in1=vr,
                                                    op0=ALU.mult, op1=ALU.add))
                step(nc.vector.tensor_scalar(mn, mn, 0.5, None, ALU.mult))

            def norm_params(a, b):
                moments(step, stats[:, a:b, :], mean[:, a:b], var[:, a:b], tmp[:, a:b])
                step(nc.vector.tensor_scalar(var[:, a:b], var[:, a:b], 1.0 / D, EPS, ALU.mult, ALU.add))
                rsqrt(step, var[:, a:b], rstd[:, a:b], tmp[:, a:b])

            def norm_x(i, e):
                if not real(i):
                    return
                if some(i - 1):
                    dve.wait_ge(tr_done, i - 1)
                nc.vector.tensor_scalar(xn[e][:, :], x_all[:, i, :], mean[:, bass.ds(i, 1)], rstd[:, bass.ds(i, 1)],
                                        ALU.subtract, ALU.mult).then_inc(xn_ready, 1)

            dve.wait_ge(x_in[0], 16)
            for i in range(X0):
                step(nc.vector.bn_stats(stats[:, i, :], x_all[:, i, :]))
            norm_params(0, X0)
            norm_x(0, 0)
            norm_x(1, 1)
            for e in range(2):
                step(nc.vector.memset(v_hi[e][:, :, :, :, :], 0.0))
                nc.vector.memset(v_lo[e][:, :, :, :, :], 0.0).then_inc(v_init, 2)
                for b in range(2):
                    r = slice(64 * b, 64 * b + 64)
                    nc.vector.memset(v_hi[e][r, :, :, b, 8:9].rearrange("p n j v -> p (n j) v"), 1.0).then_inc(v_init, 1)
            nc.vector.tensor_copy(ident_bf[:, :], ident[:, :]).then_inc(consts_ok, 1)

            def qk_low(i, e):
                if not real(i):
                    return
                dve.wait_ge(qk_hi, 2 * i + 2)
                if some(i - 1):
                    dve.wait_ge(qm_ready, 2 * (i - 1))
                    dve.wait_ge(scored, NG * (i - 1))
                nc.vector.scalar_tensor_tensor(out=q_lo[e][:, :], in0=m2_ps[:, 0:2 * P], scalar=QK_SCALE,
                                               in1=q_hi[e][:, :], op0=ALU.mult, op1=ALU.subtract).then_inc(qk_lo, 1)
                nc.vector.tensor_tensor(k_lo[e][:, :, :].rearrange("p h t -> p (h t)"), m2_ps[:, 2 * P:4 * P],
                                        k_hi[e][:, :, :].rearrange("p h t -> p (h t)"), ALU.subtract).then_inc(qk_lo, 1)

            def v_low(i, e):
                if not real(i):
                    return
                dve.wait_ge(v_hi_out, 2 * i + 2)
                if some(i - 1):
                    dve.wait_ge(pv_done, NG * (i - 1))
                for b in range(2):
                    r = slice(64 * b, 64 * b + 64)
                    nc.vector.tensor_tensor(v_lo[e][r, :, :, b, 0:8].rearrange("p n j v -> p (n j) v"),
                                            m_ps[r, 2 * P:3 * P].rearrange("p (n v) -> p n v", v=DH),
                                            v_hi[e][r, :, :, b, 0:8].rearrange("p n j v -> p (n j) v"),
                                            ALU.subtract).then_inc(v_lo_out, 1)

            def add_mask(i, e, g, nth):
                if not real(i):
                    return
                n = NG * i + g
                dve.wait_ge(scored, n + 1)
                if g == 0:
                    dve.wait_ge(mask_in[e], 32 * nth)
                if some(n - 7):
                    dve.wait_ge(low, n - 7)
                m = mask_sb[e][:, g, :, :, :].rearrange("p r b k -> p r (b k)").unsqueeze(2).to_broadcast([P, 2, 2, P])
                nc.vector.tensor_tensor(prob[4 * e + g][:, :, :, :].rearrange("p (r h) b k -> p r h (b k)", r=2),
                                        sc_ps[g % 2][:, :].rearrange("p (r h k) -> p r h k", r=2, h=2),
                                        m, ALU.add).then_inc(masked, 1)

            def row_max(i, e, g):
                if not real(i):
                    return
                n = NG * i + g
                dve.wait_ge(masked, n + 1)
                nc.vector.tensor_reduce(rowmax[g][:, :], prob[4 * e + g][:, :, :, :].rearrange("p a b k -> p (a b) k"),
                                        AX.X, ALU.max).then_inc(maxed, 1)

            def shift(i, e, g):
                if not real(i):
                    return
                n = NG * i + g
                dve.wait_ge(maxed, n + 1)
                pr = prob[4 * e + g][:, :, :, :].rearrange("p a b k -> p (a b) k")
                nc.vector.tensor_tensor(pr, pr, rowmax[g][:, :].unsqueeze(2).to_broadcast([P, 8, S]),
                                        ALU.subtract).then_inc(shifted, 1)

            def sums_out(i, e, g):
                if not real(i):
                    return
                m = g // 2
                dve.wait_ge(pv_done, NG * i + g + 1)
                src = o_ps[m][64:128, 0:288].rearrange("p (n v) -> p n v", v=36)[:, :, 18:36]
                dst = os_all[64:128, bass.ds(i, 1), :].rearrange("p i (b n v) -> p (i n) b v", b=2, v=9)
                nc.vector.tensor_copy(dst[:, 8 * m:8 * m + 8, :, :], src.rearrange("p n (b v) -> p n b v", b=2)).then_inc(o_out_v, 1)

            def tile_steps(t, e):
                i = 2 * t + e
                for g in range(NG):
                    add_mask(i, e, g, t + 1)
                    row_max(*unit(i, e, g, 1))
                    shift(*unit(i, e, g, SHIFT_LAG))
                    if g % 2 == 0:
                        sums_out(*unit(i, e, g, OUT_LAG))
                    if g == 0:
                        v_low(i - 1, 1 - e)
                    if g == 1:
                        qk_low(i + 1, 1 - e)
                    if g == 2:
                        norm_x(i + 2, e)

            qk_low(0, 0)
            dve.wait_ge(x_in[1], 16)
            for i in range(X0, NT):
                nc.vector.bn_stats(stats[:, i, :], x_all[:, i, :]).then_inc(dve_own, 1)
            own[0] += NT - X0
            dve.wait_ge(dve_own, own[0])
            norm_params(X0, NT)
            dve.wait_ge(lam_in_s, N_LAM)
            for a in range(2):
                step(nc.vector.tensor_tensor(lam_prod[:, a, :], lam_in[:, 2 * a, :], lam_in[:, 2 * a + 1, :], ALU.mult))
            nc.vector.tensor_reduce(lam_sum[:, :, :].rearrange("p a h -> p (a h)"),
                                    lam_prod[:, :, :].rearrange("p a (h d) -> p (a h) d", d=DH),
                                    AX.X, ALU.add).then_inc(lam_sums, 1)
            for t in range(2):
                tile_steps(t, 0)
                tile_steps(t, 1)
            with dve.Fori(2, NT // 2 - 1) as t:
                tile_steps(t, 0)
                tile_steps(t, 1)
            for t in range(NT // 2 - 1, NT // 2 + 1):
                tile_steps(t, 0)
                tile_steps(t, 1)

            for a in range(3):
                r = slice(32 * a, 32 * a + 32)
                nc.vector.tensor_copy(spread[r, :].rearrange("p (e f) -> p e f", e=E),
                                      ident[r, r].unsqueeze(2).to_broadcast([E, E, F])).then_inc(consts_ok, 1)
            dve.wait_ge(lam_exps, 1)
            step(nc.vector.tensor_tensor(lam_all[:, :], lam_exp[:, 0, :], lam_exp[:, 1, :], ALU.subtract))
            step(nc.vector.tensor_scalar(lam_all[:, :], lam_all[:, :], LAMBDA_INIT, None, ALU.add))
            for j in range(2):
                r = slice(64 * j, 64 * j + 64)
                for b in range(2):
                    step(nc.vector.tensor_copy(lam[r, b, :], lam_all[r, :].rearrange("p (n j) -> p n j", j=2)[:, :, j]))
            dve.wait_ge(sel_hi_ok, 1)
            nc.vector.tensor_tensor(sel_lo[:, :], t_ps[:, 0:E], sel_hi[:, :], ALU.subtract).then_inc(sel_lo_ok, 1)

            class Chain:
                SEQ = 46

                def __init__(self, c):
                    self.base, self.n = c * self.SEQ, 0

                def add(self, ins):
                    self.n += 1
                    ins.then_inc(dve_seq, 1)

                def wait(self):
                    dve.wait_ge(dve_seq, self.base + self.n)

                def __call__(self, ins):
                    self.add(ins)
                    self.wait()

            class Own(Chain):
                def __init__(self):
                    pass

                def add(self, ins):
                    own[0] += 1
                    ins.then_inc(dve_own, 1)

                def wait(self):
                    dve.wait_ge(dve_own, own[0])

            def inverse_sums(c, ch):
                if some(c):
                    dve.wait_ge(sq_done, c)
                os_c = os_all[:, bass.ts(c, TC), :].rearrange("p i (n v) -> p (i n) v", v=9)
                ch(nc.vector.reciprocal(linv[:, :, :].rearrange("p n h -> p (n h)").unsqueeze(2), os_c[:, :, 8:9]))
                lv = linv[:, :, 1].rearrange("p (i n) -> p i n", i=TC)
                lm = lam[:, :, :].rearrange("p b n -> p (b n)").unsqueeze(1).to_broadcast([P, TC, 2 * HP])
                nc.vector.tensor_tensor(lv, lv, lm, ALU.mult).then_inc(inv_done, 1)

            def mean_squares(c, ch):
                dve.wait_ge(sq_done, c + 1)
                if some(c):
                    dve.wait_ge(on_done, c)
                ch(nc.vector.tensor_reduce(sq_v[:, 0:64], osq[:, :, :], AX.X, ALU.add))
                ch.add(nc.vector.tensor_scalar(sq_v[:, 0:64], sq_v[:, 0:64], 1.0 / DH, EPS, ALU.mult, ALU.add))

            def residual(c, ch):
                dve.wait_ge(wo_done, c + 1)
                for b in range(2):
                    r = slice(64 * b, 64 * b + 64)
                    xr = x_all[r, bass.ts(c, TC), :].rearrange("p i d -> p (i d)")
                    ch.add(nc.vector.tensor_tensor(xr, xr, w_ps[b][r, :], ALU.add))
                ch.wait()
                nc.vector.tensor_copy(sq_w[:, 0:1], sq_v[:, 0:1]).then_inc(res_done, 1)

            def token_stats(c, ch):
                for ii in range(TC):
                    ch.add(nc.vector.bn_stats(fstats[:, ii, :], x_all[:, bass.ds(c * TC + ii, 1), :].rearrange("p i d -> p (i d)")))
                ch.wait()

            def variances(c, ch):
                ch(nc.vector.tensor_scalar(sq_v[:, 64:64 + TC], fvar[:, :], 1.0 / D, EPS, ALU.mult, ALU.add))

            def normalise(c, ch):
                if some(c):
                    dve.wait_ge(ftr_done, c)
                for ii in range(TC):
                    ins = nc.vector.tensor_scalar(fn[:, ii, :], x_all[:, bass.ds(c * TC + ii, 1), :].rearrange("p i d -> p (i d)"),
                                                  fmean[:, ii:ii + 1], sq_y[:, 64 + ii:65 + ii], ALU.subtract, ALU.mult)
                    if ii < TC - 1:
                        ch.add(ins)
                ch.wait()
                ins.then_inc(fn_done, 1)

            def norm_low(c, r, ch):
                dve.wait_ge(fnh_out, c + 1)
                if some(c - 1):
                    dve.wait_ge(h_done, FT * (c - 1))
                nc.vector.tensor_tensor(fn_lo[r][:, :], t_ps[:, :], fn_hi[r][:, :], ALU.subtract).then_inc(fnl_out, 1)

            def sigmoid(c, ch):
                dve.wait_ge(lg_out, 2 * c + 2)
                ch(nc.vector.tensor_scalar(sig[:, :, :], sig[:, :, :], 1.0, None, ALU.add))
                ch.add(nc.vector.reciprocal(sig[:, :, :], sig[:, :, :]))

            def choose(c, ch):
                for ii in range(TC):
                    ch.add(nc.vector.max(top8[:, ii, :], logit[:, ii, :]))
                ch.wait()
                ch(nc.vector.memset(top8[:, :, TOPK:8], NOMATCH))
                dve.nop(nofuse=True)
                for ii in range(TC):
                    ch.add(nc.vector.match_replace(rest[:, ii, :], top8[:, ii, :], logit[:, ii, :], HIDE))
                ch.wait()

            def gate_parts(c, ch):
                ch(nc.vector.tensor_tensor(gate[:, :, :], rest[:, :, :], logit[:, :, :], ALU.not_equal))
                ch(nc.vector.tensor_tensor(gate[:, :, :], gate[:, :, :], sig[:, :, :], ALU.mult))
                if some(c):
                    dve.wait_ge(gtr_done, c)
                ch(nc.vector.tensor_copy(gpart[:, :, 0, :], gate[:, :, :]))
                ch(nc.vector.tensor_tensor(gate[:, :, :], gate[:, :, :], gpart[:, :, 0, :], ALU.subtract))
                ch(nc.vector.tensor_copy(gpart[:, :, 1, :], gate[:, :, :]))
                nc.vector.tensor_tensor(gpart[:, :, 2, :], gate[:, :, :], gpart[:, :, 1, :], ALU.subtract).then_inc(parts_done, 1)

            def apply_gate(c, f):
                n = FT * c + f
                dve.wait_ge(relu_done, n + 1)
                dve.wait_ge(g_done, n + 1)
                if some(n - 3):
                    dve.wait_ge(gh_low, n - 3)
                nc.vector.tensor_tensor(ghid[f % 4][:, :], g_ps[f % 2][:, :], hid[f % 2][:, :], ALU.mult).then_inc(gated, 1)

            def final_add(c, r, stores):
                dve.wait_ge(y_turned, c + 1)
                if some(stores):
                    dve.wait_ge(stored[r], stores)
                nc.vector.tensor_tensor(y_sb[r][:, :, :].rearrange("p i d -> p (i d)"),
                                        x_all[:, bass.ts(c, TC), :].rearrange("p i d -> p (i d)"), w_ps[0][:, :],
                                        ALU.add).then_inc(y_sum, 1)

            allv, ally, allw = sq_v[:, :], sq_y[:, :], sq_w[:, :]

            def chunk(c, r, part1, part2, stores):
                ch = Chain(c)
                for f in range(FT):
                    apply_gate(c, f)
                    if part1 and f == 0:
                        inverse_sums(c + 2, ch)
                    if part2 and f == 1:
                        dve.nop(nofuse=True)
                        token_stats(c + 1, ch)
                    if part2 and f == 2:
                        moments(ch, fstats, fmean[:, :], fvar[:, :], ftmp[:, :])
                    if f == 4 and some(c):
                        final_add(c - 1, 1 - r, stores)
                    if part1 and f == 5:
                        mean_squares(c + 2, ch)
                    if part2 and f == 5:
                        variances(c + 1, ch)
                        rsqrt(ch, allv, ally, allw, 1)
                    if part2 and f == 6:
                        newton(ch, allv, ally, allw)
                        newton(ch, allv, ally, allw)
                        nc.vector.tensor_copy(sq_w[:, 0:1], sq_y[:, 0:1]).then_inc(rr_done, 1)
                    if part2 and f == 7:
                        normalise(c + 1, ch)
                    if part2 and f == 9:
                        norm_low(c + 1, 1 - r, ch)
                    if part2 and f == 11:
                        sigmoid(c + 1, ch)
                    if part2 and f == 12:
                        choose(c + 1, ch)
                    if part2 and f == 13:
                        gate_parts(c + 1, ch)
                    if part1 and f == 14:
                        residual(c + 2, ch)
                assert not (part1 and part2) or ch.n == Chain.SEQ, ch.n

            one = Own()
            dve.wait_ge(o_out_a, NU // 2)
            dve.wait_ge(o_out_v, NU // 2)
            inverse_sums(0, one)
            mean_squares(0, one)
            one.wait()
            rsqrt(one, sq_v[:, 0:64], sq_y[:, 0:64], sq_w[:, 0:64])
            nc.vector.tensor_copy(sq_w[:, 0:1], sq_y[:, 0:1]).then_inc(rr_done, 1)
            inverse_sums(1, one)
            residual(0, one)
            token_stats(0, one)
            moments(one, fstats, fmean[:, :], fvar[:, :], ftmp[:, :])
            mean_squares(1, one)
            variances(0, one)
            rsqrt(one, allv, ally, allw)
            nc.vector.tensor_copy(sq_w[:, 0:1], sq_y[:, 0:1]).then_inc(rr_done, 1)
            normalise(0, one)
            norm_low(0, 0, one)
            sigmoid(0, one)
            choose(0, one)
            gate_parts(0, one)
            residual(1, one)
            chunk(0, 0, True, True, 0)
            chunk(1, 1, True, True, 0)
            with dve.Fori(1, NC // 2 - 1) as u:
                chunk(2 * u, 0, True, True, 16 * u - 16)
                chunk(2 * u + 1, 1, True, True, 16 * u)
            chunk(NC - 2, 0, False, True, 16 * (NC // 2 - 2))
            chunk(NC - 1, 1, False, False, 16 * (NC // 2 - 1))
            final_add(NC - 1, 1, 16 * (NC // 2 - 1))


_INS = ['x', 'ctx_1024', 'mask_Bx16xSxS2_ff0', 'L0_xattn_W_q', 'L0_xattn_W_k', 'L0_xattn_W_v', 'L0_xattn_W_o',
        'L0_xattn_lambda_q1', 'L0_xattn_lambda_k1', 'L0_xattn_lambda_q2', 'L0_xattn_lambda_k2',
        'L0_xattn_rms_scale', 'L0_ffn_expert_sel', 'L0_ffn_keys', 'L0_ffn_values']
_OUTS = [((B, S, D), 'float32')]


def kernel(**inputs):
    import numpy as _np
    import concourse.bacc as _bacc
    from concourse import mybir as _mybir
    from concourse.bass_utils import run_bass_kernel_spmd as _run

    nc = _bacc.Bacc("TRN2", target_bir_lowering=False, num_devices=1)
    arrays, args = {}, []
    for name in _INS:
        a = _np.ascontiguousarray(inputs[name])
        arrays[f"in_{name}_dram"] = a
        args.append(nc.dram_tensor(f"in_{name}_dram", a.shape, _mybir.dt.from_np(a.dtype), kind="ExternalInput").ap())
    for i, (shape, dtype) in enumerate(_OUTS):
        dt = _mybir.dt.from_np(_np.dtype(dtype))
        args.append(nc.dram_tensor(f"out_{i}_dram", shape, dt, kind="ExternalOutput").ap())
    xattn_ffn(nc, *args)
    r = _run(nc, [arrays], core_ids=[0])
    return r.results[0]["out_0_dram"]
```

```python
from contextlib import ExitStack

import concourse.bass as bass
from concourse import mybir

ALU = mybir.AluOpType
ACT = mybir.ActivationFunctionType
AX = mybir.AxisListType
F32 = mybir.dt.float32
F16 = mybir.dt.float16
BF16 = mybir.dt.bfloat16
I32 = mybir.dt.int32

P = 128
B, S, D = 64, 64, 128
H, DH = 16, 8
E, F, TOPK = 32, 64, 4
LAMBDA_INIT = 0.8
EPS = 1e-5
QK_SCALE = DH ** -0.5
NT = B * S // P
NG = 4
NU = NT * NG
HP = H // 2
NC = 8
TC = NT // NC
CW = TC * P
FT = E * F // P
EPT = P // F
KW, VW = E * F, FT * D
PIECE = 640
OW = 2 * HP * 2 * 9
RSQRT_MAGIC = float(0x5F3759DF)
HIDE = -3.0e38
NOMATCH = 3.0e38

DOWN_LAG = 4

SHIFT_LAG = 2
EXP_LAG = 3
TURN_LAG = 4
SPLIT_LAG = 5
PLAIN = 3
PLAIN_LAG = 6
PV_LAG = 7
OUT_LAG = 8
TB = 4
NB = NT // TB


def some(v):
    return not isinstance(v, int) or v > 0


def unit(i, e, g, lag):
    back, g2 = divmod(g - lag, NG)
    return i + back, (e + back) % TB, g2


def tile(i, e, ahead):
    return i + ahead, (e + ahead) % TB


def has(c, ahead):
    return not isinstance(c, int) or 0 <= c + ahead < NC


def real(i):
    return not isinstance(i, int) or 0 <= i < NT


def xattn_ffn(nc, x, ctx_in, mask, W_q, W_k, W_v, W_o, lq1, lk1, lq2, lk2, rms_scale,
              expert_sel, keys, values, out):
    with ExitStack() as stack:
        def sb(name, shape, dt=F32):
            return stack.enter_context(nc.sbuf_tensor(name, shape, dt))

        def sem(name):
            return stack.enter_context(nc.semaphore(name))

        ident = sb("ident", [P, P])
        ident_h = sb("ident_h", [P, P], F16)
        ident_bf = sb("ident_bf", [P, P], BF16)
        head_cols = sb("head_cols", [P, NG])
        spread = sb("spread", [96, E * F], BF16)
        wq_raw = sb("wq_raw", [P, 2 * P])
        wk_raw = sb("wk_raw", [P, 2 * P])
        wq = sb("wq", [P, 2, P])
        wk = sb("wk", [P, 2, P])
        wv = sb("wv", [P, P])
        wo_raw = sb("wo_raw", [P, 2, D])
        wo = sb("wo", [P, 2, D])
        rms_col = sb("rms_col", [P, 1])
        rms_scaled = sb("rms_scaled", [P, 1])
        sel_rows = sb("sel_rows", [E, D])
        sel_hi = sb("sel_hi", [P, E], F16)
        sel_lo = sb("sel_lo", [P, E], F16)
        ew = sb("ew", [P, KW + VW])
        ew_hi = sb("ew_hi", [P, KW + VW], F16)
        ew_lo = sb("ew_lo", [P, KW + VW], F16)
        keys_hi, values_hi = ew_hi[:, 0:KW], ew_hi[:, KW:]
        keys_lo, values_lo = ew_lo[:, 0:KW], ew_lo[:, KW:]
        lam_in = sb("lam_in", [P, 4, H * DH])
        lam_prod = sb("lam_prod", [P, 2, H * DH])
        lam_sum = sb("lam_sum", [P, 2, H])
        lam_exp = sb("lam_exp", [P, 2, H])
        lam_all = sb("lam_all", [P, H])
        lam = sb("lam", [P, 2, HP])

        x_all = sb("x_all", [P, NT, D])
        os_all = sb("os_all", [P, NT, OW])
        stats = sb("stats", [P, NT, 6])
        var = sb("var", [P, NT])
        tmp = sb("tmp", [P, NT])
        mean = sb("mean", [P, NT])
        rstd = sb("rstd", [P, NT])

        mask_sb = [sb(f"mask_sb{e}", [P, NG, 2, 2, S]) for e in range(2)]
        ctx_sb = [sb(f"ctx_sb{e}", [P, D]) for e in range(TB)]
        xn = [sb(f"xn{e}", [P, D]) for e in range(2)]
        xc_t = [sb(f"xc_t{e}", [P, 2, P]) for e in range(2)]
        q_hi = [sb(f"q_hi{e}", [P, 2 * P], F16) for e in range(2)]
        q_lo = [sb(f"q_lo{e}", [P, 2 * P], F16) for e in range(2)]
        k_hi = [sb(f"k_hi{e}", [P, 2, P], F16) for e in range(2)]
        k_lo = [sb(f"k_lo{e}", [P, 2, P], F16) for e in range(2)]
        qm_hi = [sb(f"qm_hi{e}", [P, 4, NG, S], F16) for e in range(2)]
        qm_lo = [sb(f"qm_lo{e}", [P, 4, NG, S], F16) for e in range(2)]
        v_hi = [sb(f"v_hi{e}", [P, HP, 2, 2, 9], F16) for e in range(TB)]
        v_lo = [sb(f"v_lo{e}", [P, HP, 2, 2, 9], F16) for e in range(TB)]
        prob = [sb(f"prob{r}", [P, 4, 2, S]) for r in range(8)]
        rowmax = [sb(f"rowmax{r}", [P, 8]) for r in range(4)]
        p_hi = [sb(f"p_hi{r}", [P, 4, P], F16) for r in range(NG)]
        p_lo = [sb(f"p_lo{r}", [P, 4, P], F16) for r in range(NG)]
        p_t = [sb(f"p_t{r}", [P, 4 * P]) for r in range(2)]

        linv = sb("linv", [P, 64, 2])
        om = sb("om", [P, 64, 2, 8])
        oc = sb("oc", [P, 64, 8])
        osq = sb("osq", [P, 64, 8])
        on = sb("on", [P, 64, 8])
        sq_v = sb("sq_v", [P, 64 + TC])
        sq_y = sb("sq_y", [P, 64 + TC])
        sq_w = sb("sq_w", [P, 64 + TC])
        o_t = sb("o_t", [P, CW])
        fstats = sb("fstats", [P, TC, 6])
        fmean = sb("fmean", [P, TC])
        fvar = sb("fvar", [P, TC])
        ftmp = sb("ftmp", [P, TC])
        fn = sb("fn", [P, TC, D])
        fn_hi = [sb(f"fn_hi{r}", [P, CW], F16) for r in range(2)]
        fn_lo = [sb(f"fn_lo{r}", [P, CW], F16) for r in range(2)]
        logit = sb("logit", [P, TC, E])
        sig = sb("sig", [P, TC, E])
        top8 = sb("top8", [P, TC, 8])
        rest = sb("rest", [P, TC, E])
        gate = sb("gate", [P, TC, E])
        gpart = sb("gpart", [P, TC, 3, E], BF16)
        gate_t = [sb(f"gate_t{r}", [96, CW], BF16) for r in range(2)]
        flat = [prob[r][:, :, :, :].rearrange("p a b k -> p (a b k)") for r in range(8)]
        ghid, hid = flat[0:4], flat[4:8]
        gh_hi = [p_hi[r][:, :, :].rearrange("p a k -> p (a k)") for r in range(4)]
        gh_lo = [p_lo[r][:, :, :].rearrange("p a k -> p (a k)") for r in range(4)]
        gh_hi += [sb(f"gh_hi{r}", [P, CW], F16) for r in range(4, 8)]
        gh_lo += [sb(f"gh_lo{r}", [P, CW], F16) for r in range(4, 8)]
        y_t = sb("y_t", [P, CW])

        bank = [stack.enter_context(nc.psum_tensor(f"bank{r}", [P, 512], F32)) for r in range(8)]
        sc_ps, pt_ps, o_ps, m_ps, m2_ps = bank[0:2], bank[2:4], bank[4:6], bank[6], bank[7]
        w_ps, y_ps, h_ps, g_ps, t_ps = bank[0], (bank[1], bank[6]), bank[2:4], bank[4:6], bank[7]

        x_in = [sem("x_in0"), sem("x_in1")]
        w_in = sem("w_in")
        lam_in_s = sem("lam_in_s")
        wp_in = sem("wp_in")
        ew_in = sem("ew_in")
        sel_in = sem("sel_in")
        mask_in = [sem(f"mask_in{e}") for e in range(2)]
        ctx_in_s = [sem(f"ctx_in{e}") for e in range(TB)]
        ident0 = sem("ident0")
        ident_ok = sem("ident_ok")
        dve_own = sem("dve_own")
        heads_ok = sem("heads_ok")
        consts_ok = sem("consts_ok")
        w_perm = sem("w_perm")
        rms_ok = sem("rms_ok")
        wo_ok = sem("wo_ok")
        sel_turned = sem("sel_turned")
        sel_hi_ok = sem("sel_hi_ok")
        sel_lo_ok = sem("sel_lo_ok")
        spread_ok = sem("spread_ok")
        ew_hi_ok = sem("ew_hi_ok")
        ew_lo_ok = sem("ew_lo_ok")
        lam_sums = sem("lam_sums")
        lam_exps = sem("lam_exps")
        v_init = sem("v_init")
        xn_ready = sem("xn_ready")
        tr_done = sem("tr_done")
        xt_ready = sem("xt_ready")
        qk_done = sem("qk_done")
        vp_done = sem("vp_done")
        qk_hi = sem("qk_hi")
        qk_lo = sem("qk_lo")
        v_hi_out = sem("v_hi_out")
        v_lo_out = sem("v_lo_out")
        qm_hi_ok = sem("qm_hi_ok")
        qm_lo_ok = sem("qm_lo_ok")
        scored = sem("scored")
        masked = sem("masked")
        maxed = sem("maxed")
        shifted = sem("shifted")
        exped = sem("exped")
        high = sem("high")
        plain = sem("plain")
        low_v = sem("low_v")
        low_p = sem("low_p")
        turned = sem("turned")
        pv_done = sem("pv_done")
        o_out = sem("o_out")
        inv_own = sem("inv_own")
        inv_done = sem("inv_done")
        pool_own = sem("pool_own")
        sq_done = sem("sq_done")
        rr_done = sem("rr_done")
        on_done = sem("on_done")
        otr_done = sem("otr_done")
        ot_out = sem("ot_out")
        wo_done = sem("wo_done")
        res_done = sem("res_done")
        fn_done = sem("fn_done")
        ftr_done = sem("ftr_done")
        fnh_out = sem("fnh_out")
        fnl_out = sem("fnl_out")
        lg_done = sem("lg_done")
        lg_out = sem("lg_out")
        parts_done = sem("parts_done")
        gtr_done = sem("gtr_done")
        gt_out = sem("gt_out")
        y_out = sem("y_out")
        y_turned = sem("y_turned")
        y_sum = sem("y_sum")
        stored = sem("stored")
        dve_seq = sem("dve_seq")
        h_done = sem("h_done")
        g_done = sem("g_done")
        relu_done = sem("relu_done")
        gated = sem("gated")
        gh_high = sem("gh_high")
        gh_low = sem("gh_low")
        used = sem("used")

        x_v = x.rearrange("b s d -> (b s) d").rearrange("(i p) d -> p i d", p=P)
        out_v = out.rearrange("b s d -> (b s) d").rearrange("(i p) d -> p i d", p=P)
        ctx_v = ctx_in.rearrange("b s d -> (b s) d").rearrange("(i p) d -> p i d", p=P)
        mask_v = mask.rearrange("b (n j) q k -> (j q) b n k", j=2)

        X0 = 4
        N_W = 16 * 3
        N_LAM = 16 * 4
        N_EW = 16 * 2
        N_WP = 16 * (2 * 2 * HP)

        block = stack.enter_context(nc.Block())

        @block.sync
        def _(sp):
            def load_mask(i, e):
                for b in range(2):
                    sp.dma_start(mask_sb[e][:, :, :, b, :].rearrange("p g r k -> p (g r) k"),
                                 mask_v[:, 2 * i + b]).then_inc(mask_in[e], 16)

            def load_ctx(i, e):
                sp.dma_start(ctx_sb[e][:, :], ctx_v[:, i, :]).then_inc(ctx_in_s[e], 16)

            def next_loads(i, e):
                if real(i + 2):
                    if some(i - 1):
                        sp.wait_ge(tr_done, i - 1)
                    load_ctx(i + 2, (e + 2) % TB)
                if some(i - 1):
                    sp.wait_ge(masked, NG * (i - 1))
                load_mask(i, e % 2)

            sp.dma_start(x_all[:, 0:X0, :], x_v[:, 0:X0, :]).then_inc(x_in[0], 16)
            load_ctx(0, 0)
            sp.dma_start(wq_raw[:, :], W_q).then_inc(w_in, 16)
            sp.dma_start(wk_raw[:, :], W_k).then_inc(w_in, 16)
            sp.dma_start(wv[:, :], W_v).then_inc(w_in, 16)
            load_ctx(1, 1)
            sp.dma_start(sel_rows[:, :], expert_sel).then_inc(sel_in, 16)
            next_loads(0, 0)
            sp.dma_start(x_all[:, X0:NT, :], x_v[:, X0:NT, :]).then_inc(x_in[1], 16)
            next_loads(1, 1)
            for a in range(4):
                src = (lq1, lk1, lq2, lk2)[a].rearrange("(o h) d -> o (h d)", o=1)
                sp.dma_start(lam_in[:, a, :], src.to_broadcast([P, H * DH])).then_inc(lam_in_s, 16)
            sp.dma_start(ew[:, 0:KW].rearrange("d (e f) -> d e f", e=E),
                         keys.rearrange("e d f -> d e f")).then_inc(ew_in, 16)
            sp.dma_start(ew[:, KW:].rearrange("p (t d) -> p t d", t=FT),
                         values.rearrange("(t e) f d -> (e f) t d", e=EPT)).then_inc(ew_in, 16)
            for i in range(2, 7):
                next_loads(i, i % TB)
            next_loads(7, 3)
            with sp.Fori(2, NB - 1) as t:
                for e in range(TB):
                    next_loads(TB * t + e, e)
            for b in range(2):
                for hp in range(HP):
                    r0 = (HP * b + hp) * DH
                    src = W_o.rearrange("(hp j d) n -> hp d j n", j=2, d=DH)[hp]
                    sp.dma_start(wo_raw[r0:r0 + DH, :, :], src).then_inc(wp_in, 16)
                    sp.dma_start(rms_col[r0:r0 + DH, :],
                                 rms_scale.rearrange("(d o) -> d o", o=1)).then_inc(wp_in, 16)
                next_loads(NT - TB + b, b)
            for e in range(2, TB):
                next_loads(NT - TB + e, e)

        @block.gpsimd
        def _(pool):
            nc.gpsimd.memset(ident[:, :], 0.0).then_inc(ident0, 1)
            pool.wait_ge(ident0, 1)
            nc.gpsimd.affine_select(out=ident[:, :], in_=ident[:, :], compare_op=ALU.not_equal, fill=1.0,
                                    base=0, pattern=[[-1, P]], channel_multiplier=1).then_inc(ident_ok, 1)
            for e in range(TB):
                nc.gpsimd.memset(v_lo[e][:, :, :, :, :], 0.0).then_inc(v_init, 1)
                nc.gpsimd.memset(v_hi[e][:, :, :, :, :], 0.0).then_inc(v_init, 1)
            pool.wait_ge(v_init, 2 * TB)
            for e in range(TB):
                for b in range(2):
                    r = slice(64 * b, 64 * b + 64)
                    nc.gpsimd.memset(v_hi[e][r, :, :, b, 8:9].rearrange("p n j v -> p (n j) v"), 1.0).then_inc(v_init, 1)

            def weights_low(t, cols):
                pool.wait_ge(ew_hi_ok, t)
                nc.gpsimd.tensor_tensor(ew_lo[:, cols], ew[:, cols], ew_hi[:, cols], ALU.subtract).then_inc(ew_lo_ok, 1)

            pool.wait_ge(heads_ok, 1)

            def one_head(i, e, h):
                if not real(i):
                    return
                pool.wait_ge(qk_lo, 2 * i + 1)
                if some(i - 1):
                    pool.wait_ge(scored, NG * (i - 1))
                kept = head_cols[:, :].unsqueeze(1).unsqueeze(3).to_broadcast([P, 2, NG, S])
                src = q_lo[e % 2][:, h * P:(h + 1) * P].rearrange("p (n s) -> p n s", n=2).unsqueeze(2)
                nc.gpsimd.tensor_tensor(qm_lo[e % 2][:, 2 * h:2 * h + 2, :, :], src.to_broadcast([P, 2, NG, S]), kept,
                                        ALU.mult).then_inc(qm_lo_ok, 1)

            def shift(i, e, g):
                if not real(i):
                    return
                pool.wait_ge(maxed, NG * i + g + 1)
                pr = prob[4 * (e % 2) + g][:, :, :, :].rearrange("p a b k -> p (a b) k")
                nc.gpsimd.tensor_tensor(pr, pr, rowmax[g][:, :].unsqueeze(2).to_broadcast([P, 8, S]),
                                        ALU.subtract).then_inc(shifted, 1)

            def plain_low(i, e):
                if not real(i):
                    return
                pool.wait_ge(plain, i + 1)
                nc.gpsimd.tensor_tensor(p_lo[PLAIN][:, :, :].rearrange("p a k -> p (a k)"), p_t[e % 2][:, :],
                                        p_hi[PLAIN][:, :, :].rearrange("p a k -> p (a k)"),
                                        ALU.subtract).then_inc(low_p, 1)

            def heads(c, part):
                os_c = os_all[:, bass.ts(c, TC), :].rearrange("p i (n v) -> p (i n) v", v=9)
                if part < 2:
                    pool.wait_ge(inv_done, c + 1)
                    if some(c):
                        pool.wait_ge(on_done, c)
                    half = slice(P // 2 * part, P // 2 * part + P // 2)
                    inv = linv[:, :, :].rearrange("p n h -> p (n h)")[:, half].unsqueeze(2).to_broadcast([P, P // 2, 8])
                    nc.gpsimd.tensor_tensor(om[:, :, :, :].rearrange("p n h v -> p (n h) v")[:, half, :],
                                            os_c[:, half, 0:8], inv, ALU.mult).then_inc(pool_own, 1)
                if part == 2:
                    pool.wait_ge(pool_own, 3 * c + 2)
                    nc.gpsimd.tensor_tensor(oc[:, :, :], om[:, :, 0, :], om[:, :, 1, :], ALU.subtract).then_inc(pool_own, 1)
                if part == 3:
                    pool.wait_ge(pool_own, 3 * c + 3)
                    nc.gpsimd.tensor_tensor(osq[:, :, :], oc[:, :, :], oc[:, :, :], ALU.mult).then_inc(sq_done, 1)

            def scale_heads(c):
                pool.wait_ge(rr_done, c + 1)
                if some(c):
                    pool.wait_ge(otr_done, c)
                nc.gpsimd.tensor_tensor(on[:, :, :], oc[:, :, :],
                                        sq_y[:, 0:64].unsqueeze(2).to_broadcast([P, 64, 8]),
                                        ALU.mult).then_inc(on_done, 1)

            def low_hidden(c, f):
                n = FT * c + f
                pool.wait_ge(gh_high, n + 1)
                if some(n - 7):
                    pool.wait_ge(used, n - 7)
                nc.gpsimd.tensor_tensor(gh_lo[f % 8][:, :], ghid[f % 4][:, :], gh_hi[f % 8][:, :],
                                        ALU.subtract).then_inc(gh_low, 1)

            def chunk(c):
                for f in range(FT):
                    low_hidden(c, f)
                    if f == 6 and has(c, 2):
                        scale_heads(c + 2)
                    if 11 <= f < 15 and has(c, 3):
                        heads(c + 3, f - 11)

            def head_start(k):
                for c, first in enumerate((4, 13, 24)):
                    if first <= k < first + 4:
                        heads(c, k - first)
                if k == 12:
                    scale_heads(0)
                if k == 19:
                    scale_heads(1)

            def tile_steps(i, e, last=False):
                for g in range(NG):
                    if g == 3:
                        one_head(*tile(i, e, 1), 1)
                    shift(*unit(i, e, g, SHIFT_LAG))
                    i2, e2, g2 = unit(i, e, g, PLAIN_LAG)
                    if g2 == PLAIN:
                        plain_low(i2, e2)
                    if g == 2:
                        one_head(*tile(i, e, 1), 0)
                    if last:
                        head_start(i * NG + g - (NT - TB) * NG)

            one_head(0, 0, 0)
            one_head(0, 0, 1)
            for e in range(TB):
                tile_steps(e, e)
            with pool.Fori(1, NB - 1) as t:
                for e in range(TB):
                    tile_steps(TB * t + e, e)
                    if e == 0:
                        weights_low(t, bass.ts(t - 1, PIECE))
            weights_low(NB - 1, slice(PIECE * (NB - 2), KW + VW))
            for e in range(TB + 3):
                tile_steps(NT - TB + e, e % TB, True)
            pool.wait_ge(pv_done, NU)
            chunk(0)
            with pool.Fori(0, NC // 2 - 2) as u:
                chunk(2 * u + 1)
                chunk(2 * u + 2)
            for c in range(NC - 3, NC):
                chunk(c)

        @block.tensor
        def _(pe):
            def pre_turn_waits(i, e, nth):
                if not real(i):
                    return
                pe.wait_ge(xn_ready, i + 1)
                pe.wait_ge(ctx_in_s[e], 16 * nth)
                if some(i):
                    pe.wait_ge(v_lo_out, 2 * i)

            def pre_turn(i, e):
                if not real(i):
                    return
                pe.transpose(m_ps[:, 0:P], xn[e % 2][:, :], ident[:, :])
                pe.transpose(m_ps[:, P:2 * P], ctx_sb[e][:, :], ident[:, :]).then_inc(tr_done, 1)

            def project_waits(i):
                if not real(i):
                    return
                pe.wait_ge(xt_ready, i + 1)
                if some(i):
                    pe.wait_ge(qk_lo, 2 * i)

            def project_v(i, e):
                if not real(i):
                    return
                pe.matmul(m_ps[:, 2 * P:3 * P], xc_t[e % 2][:, 1, :], wv[:, :], start=True,
                          stop=True, skip_group_check=True).then_inc(vp_done, 1)

            def project_qk(i, e):
                if not real(i):
                    return
                for h in range(2):
                    pe.matmul(m2_ps[:, h * P:(h + 1) * P], wq[:, h, :], xc_t[e % 2][:, 0, :], start=(h == 0), stop=True,
                              skip_group_check=True)
                for h in range(2):
                    mm = pe.matmul(m2_ps[:, (2 + h) * P:(3 + h) * P], wk[:, h, :], xc_t[e % 2][:, 1, :],
                                   start=False, stop=True, skip_group_check=True)
                mm.then_inc(qk_done, 1)

            def scores(i, e, g):
                if not real(i):
                    return
                n = NG * i + g
                if g == 0:
                    pe.wait_ge(qm_hi_ok, NG * (i + 1))
                    pe.wait_ge(qm_lo_ok, 2 * i + 2)
                    pe.wait_ge(qk_lo, 2 * i + 2)
                if some(n - 1):
                    pe.wait_ge(masked, n - 1)
                pe.matmul(sc_ps[g % 2][:, 0:2 * P], ident_h[:, :],
                          qm_hi[e % 2][:, 0, :, :].rearrange("p j s -> p (j s)"),
                          start=True, stop=True, skip_group_check=True)
                rows = slice(32 * g, 32 * g + 32)
                for p in range(2):
                    for h in range(2):
                        for b in range(2):
                            o = ((p * 2 + h) * 2 + b) * S
                            for a, (ql, kl) in enumerate(((qm_hi, k_hi), (qm_hi, k_lo), (qm_lo, k_hi))):
                                mm = pe.matmul(sc_ps[g % 2][:, o:o + S],
                                               ql[e % 2][rows, 2 * h + b, 2 * p:2 * p + 2, :].rearrange("p j s -> p (j s)"),
                                               kl[e % 2][rows, h, b * S:b * S + S],
                                               start=(o == 0 and a == 0), stop=(a == 2), skip_group_check=True)
                mm.then_inc(scored, 1)

            def turn(i, e, g):
                if not real(i):
                    return
                n = NG * i + g
                pe.wait_ge(exped, n + 1)
                if g == 1 and some(i):
                    pe.wait_ge(plain, i)
                if g == 0 and some(i):
                    pe.wait_ge(low_v, (NG - 1) * i)
                if g >= 2:
                    pe.wait_ge(low_v, (NG - 1) * i + g - 1)
                for a in range(4):
                    mm = pe.transpose(pt_ps[g % 2][:, a * P:(a + 1) * P],
                                      prob[4 * (e % 2) + g][:, a, :, :].rearrange("p b k -> p (b k)"), ident[:, :])
                mm.then_inc(turned, 1)

            def attend(i, e, g):
                if not real(i):
                    return
                if g == PLAIN:
                    pe.wait_ge(low_p, i + 1)
                else:
                    pe.wait_ge(low_v, (NG - 1) * i + g + 1)
                if g == 0:
                    pe.wait_ge(v_lo_out, 2 * i + 2)
                pair = 2 * i + g // 2
                if g % 2 == 0 and some(pair - 1):
                    pe.wait_ge(o_out, 2 * (pair - 1))
                for p in range(2):
                    for h in range(2):
                        o = (((g % 2) * 2 + p) * 2 + h) * 36
                        for a, (pt, v) in enumerate(((p_hi, v_hi), (p_hi, v_lo), (p_lo, v_hi))):
                            mm = pe.matmul(o_ps[g // 2][:, o:o + 36], pt[g][:, 2 * p + h, :],
                                           v[e][:, 2 * g + p, :, :, :].rearrange("p j b v -> p (j b v)"),
                                           start=(g % 2 == 0 and o == 0 and a == 0), stop=(a == 2),
                                           skip_group_check=True)
                mm.then_inc(pv_done, 1)

            def turn_selectors():
                pe.wait_ge(sel_in, 16)
                pe.transpose(o_ps[0][:, 0:E], sel_rows[:, :], ident[0:E, 0:E]).then_inc(sel_turned, 1)

            def turn_heads(c):
                pe.wait_ge(on_done, c + 1)
                if some(c):
                    pe.wait_ge(lg_out, 2 * c)
                for ii in range(TC):
                    mm = pe.transpose(t_ps[:, ii * P:(ii + 1) * P],
                                      on[:, 16 * ii:16 * ii + 16, :].rearrange("p n v -> p (n v)"), ident[:, :])
                mm.then_inc(otr_done, 1)

            def project_out(c, ps=w_ps):
                pe.wait_ge(ot_out, c + 1)
                if some(c - 2):
                    pe.wait_ge(y_sum, c - 2)
                pe.nop(nofuse=True)
                for b in range(2):
                    r = slice(64 * b, 64 * b + 64)
                    for ii in range(TC):
                        for j in range(2):
                            mm = pe.matmul(ps[r, ii * P:(ii + 1) * P],
                                           o_t[r, ii * P + 64 * j:ii * P + 64 * j + 64], wo[r, j, :],
                                           start=(j == 0 and ii == 0), stop=(j == 1), skip_group_check=True)
                mm.then_inc(wo_done, 1)

            def turn_norm(c):
                pe.wait_ge(fn_done, TC * (c + 1))
                if some(c):
                    pe.wait_ge(gt_out, c)
                for ii in range(TC):
                    mm = pe.transpose(t_ps[:, ii * P:(ii + 1) * P], fn[:, ii, :], ident[:, :])
                mm.then_inc(ftr_done, 1)

            def logits(c, r):
                pe.wait_ge(fnl_out, c + 1)
                for ii in range(TC):
                    for a, (xs, ws) in enumerate(((fn_hi, sel_hi), (fn_hi, sel_lo), (fn_lo, sel_hi))):
                        mm = pe.matmul(t_ps[:, ii * E:(ii + 1) * E], xs[r][:, ii * P:(ii + 1) * P], ws[:, :],
                                       start=(ii == 0 and a == 0), stop=(a == 2), skip_group_check=True)
                mm.then_inc(lg_done, 1)

            def turn_gates(c):
                pe.wait_ge(parts_done, c + 1)
                tb = t_ps[:, :].bitcast(BF16)
                for ii in range(TC):
                    mm = pe.transpose(tb[0:96, ii * P:(ii + 1) * P],
                                      gpart[:, ii, :, :].rearrange("p a e -> p (a e)"), ident_bf[:, :])
                mm.then_inc(gtr_done, 1)

            def hidden(c, r, f):
                n = FT * c + f
                if some(n - 1):
                    pe.wait_ge(relu_done, n - 1)
                for a, (ws, xs) in enumerate(((keys_hi, fn_hi), (keys_hi, fn_lo), (keys_lo, fn_hi))):
                    mm = pe.matmul(h_ps[f % 2][:, :], ws[:, f * P:(f + 1) * P], xs[r][:, :], start=(a == 0),
                                   stop=(a == 2))
                mm.then_inc(h_done, 1)

            def spread_gate(c, r, f):
                n = FT * c + f
                if f == 0:
                    pe.wait_ge(gt_out, c + 1)
                if some(n - 1):
                    pe.wait_ge(gated, n - 1)
                pe.matmul(g_ps[f % 2][:, :], spread[:, f * P:(f + 1) * P], gate_t[r][:, :], start=True,
                          stop=True).then_inc(g_done, 1)

            def down(c, r, f):
                n = FT * c + f
                pe.wait_ge(gh_low, n + 1)
                for a, (ws, xs) in enumerate(((values_hi, gh_hi), (values_hi, gh_lo), (values_lo, gh_hi))):
                    mm = pe.matmul(y_ps[r][:, :], ws[:, f * P:(f + 1) * P], xs[f % 8][:, :],
                                   start=(f == 0 and a == 0), stop=(f == FT - 1 and a == 2))
                mm.then_inc(used, 1)

            def turn_y(c):
                pe.wait_ge(y_out, c + 1)
                if has(c, 2):
                    pe.wait_ge(res_done, 2 * (c + 3))
                for ii in range(TC):
                    mm = pe.transpose(w_ps[:, ii * P:(ii + 1) * P], y_t[:, ii * P:(ii + 1) * P], ident[:, :])
                mm.then_inc(y_turned, 1)

            def chunk(c, r):
                for f in range(FT):
                    hidden(c, r, f)
                    if f >= DOWN_LAG:
                        down(c, r, f - DOWN_LAG)
                    elif has(c, -1):
                        down(c - 1, 1 - r, FT + f - DOWN_LAG)
                    if f == 5 and has(c, -1):
                        turn_y(c - 1)
                    if f == 8 and has(c, 1):
                        turn_norm(c + 1)
                    if f == 11 and has(c, 1):
                        logits(c + 1, 1 - r)
                    if f == 13 and has(c, 2):
                        turn_heads(c + 2)
                    if f == 14 and has(c, 2):
                        project_out(c + 2)
                    if f == 15 and has(c, 1):
                        turn_gates(c + 1)
                    spread_gate(c, r, f)

            def head_start(k):
                if k == 13:
                    pe.wait_ge(qk_lo, 2 * NT)
                    turn_heads(0)
                if k == 14:
                    pe.wait_ge(wo_ok, 1)
                    pe.wait_ge(v_lo_out, 2 * NT)
                    project_out(0, m_ps)
                if k == 18:
                    turn_norm(0)
                if k == 20:
                    logits(0, 0)
                if k == 22:
                    pe.wait_ge(masked, NU)
                    turn_heads(1)
                if k == 23:
                    project_out(1)
                if k == 25:
                    turn_gates(0)

            def tile_steps(i, e, turns, last=False):
                for g in range(NG):
                    scores(i, e, g)
                    turn(*unit(i, e, g, TURN_LAG))
                    if g == 1:
                        pre_turn_waits(*tile(i, e, 2), turns + (e + 2) // TB + 1)
                    if g == 2:
                        project_waits(i + 2)
                    attend(*unit(i, e, g, PV_LAG))
                    if g == 1:
                        pre_turn(*tile(i, e, 2))
                    if g == 2:
                        project_v(*tile(i, e, 2))
                    if g == 3:
                        project_qk(*tile(i, e, 2))
                    if last:
                        head_start(i * NG + g - (NT - TB) * NG)

            pe.wait_ge(ident_ok, 1)
            pre_turn_waits(0, 0, 1)
            pre_turn(0, 0)
            pe.wait_ge(w_in, N_W)
            project_waits(0)
            project_v(0, 0)
            pe.wait_ge(w_perm, 4)
            project_qk(0, 0)
            pre_turn_waits(1, 1, 1)
            pre_turn(1, 1)
            project_waits(1)
            project_v(1, 1)
            project_qk(1, 1)
            turn_selectors()
            pe.wait_ge(sel_lo_ok, 1)
            pe.wait_ge(consts_ok, 2)
            for e in range(TB):
                tile_steps(e, e, 0)
            with pe.Fori(1, NB - 1) as t:
                for e in range(TB):
                    tile_steps(TB * t + e, e, t)
            for e in range(TB + 3):
                tile_steps(NT - TB + e, e % TB, NB - 1, True)

            pe.wait_ge(ew_lo_ok, NB - 1)
            pe.wait_ge(spread_ok, 3)
            pe.wait_ge(low_v, (NG - 1) * NT)
            pe.wait_ge(plain, NT)
            pe.wait_ge(o_out, NU)
            pe.wait_ge(v_lo_out, 2 * NT)
            chunk(0, 0)
            with pe.Fori(0, NC // 2 - 2) as u:
                chunk(2 * u + 1, 1)
                chunk(2 * u + 2, 0)
            for c in range(NC - 3, NC):
                chunk(c, c % 2)
            for f in range(FT - DOWN_LAG, FT):
                down(NC - 1, 1, f)
            turn_y(NC - 1)

        @block.scalar
        def _(act):
            act.wait_ge(ident_ok, 1)
            for a in range(3):
                r = slice(32 * a, 32 * a + 32)
                nc.scalar.copy(spread[r, :].rearrange("p (e f) -> p e f", e=E),
                               ident[r, r].unsqueeze(2).to_broadcast([E, E, F])).then_inc(spread_ok, 1)
            act.wait_ge(w_in, N_W)
            for raw, w in ((wq_raw, wq), (wk_raw, wk)):
                for h in range(2):
                    src = raw[:, :].rearrange("p (n a d) -> p n a d", n=H, a=2)[:, :, h, :]
                    nc.scalar.copy(w[:, h, :].rearrange("p (n d) -> p n d", n=H), src).then_inc(w_perm, 1)

            def pre_turn_out(i, e):
                if not real(i):
                    return
                act.wait_ge(tr_done, i + 1)
                if some(i - 1):
                    act.wait_ge(qk_done, i - 1)
                    act.wait_ge(vp_done, i - 1)
                nc.scalar.copy(xc_t[e % 2][:, :, :].rearrange("p a t -> p (a t)"), m_ps[:, 0:2 * P]).then_inc(xt_ready, 1)

            def qk_high(i, e):
                if not real(i):
                    return
                act.wait_ge(qk_done, i + 1)
                if some(i - 1):
                    act.wait_ge(scored, NG * (i - 1))
                    act.wait_ge(qk_lo, 2 * (i - 1))
                nc.scalar.mul(q_hi[e % 2][:, :], m2_ps[:, 0:2 * P], QK_SCALE).then_inc(qk_hi, 1)
                nc.scalar.copy(k_hi[e % 2][:, :, :].rearrange("p h t -> p (h t)"), m2_ps[:, 2 * P:4 * P]).then_inc(qk_hi, 1)

            def one_head(i, e, j):
                if not real(i):
                    return
                act.wait_ge(qk_hi, 2 * i + 1)
                if some(i - 1):
                    act.wait_ge(scored, NG * (i - 1))
                nc.scalar.activation(qm_hi[e % 2][:, :, j, :], q_hi[e % 2][:, :].rearrange("p (n s) -> p n s", n=4),
                                     ACT.Copy, scale=head_cols[:, j:j + 1]).then_inc(qm_hi_ok, 1)

            def v_high(i, e):
                if not real(i):
                    return
                act.wait_ge(vp_done, i + 1)
                if some(i - 3):
                    act.wait_ge(pv_done, NG * (i - 3))
                elif i == 0:
                    act.wait_ge(v_init, 4 * TB)
                for b in range(2):
                    r = slice(64 * b, 64 * b + 64)
                    nc.scalar.copy(v_hi[e][r, :, :, b, 0:8].rearrange("p n j v -> p (n j) v"),
                                   m_ps[r, 2 * P:3 * P].rearrange("p (n v) -> p n v", v=DH)).then_inc(v_hi_out, 1)

            def exponent(i, e, g):
                if not real(i):
                    return
                act.wait_ge(shifted, NG * i + g + 1)
                pr = prob[4 * (e % 2) + g][:, :, :, :].rearrange("p a b k -> p (a b k)")
                nc.scalar.activation(pr, pr, ACT.Exp).then_inc(exped, 1)

            def high_part(i, e, g):
                if not real(i):
                    return
                n = NG * i + g
                act.wait_ge(turned, n + 1)
                if some(n - 3):
                    act.wait_ge(pv_done, n - 3)
                nc.scalar.copy(p_hi[g][:, :, :].rearrange("p a k -> p (a k)"), pt_ps[g % 2][:, :]).then_inc(high, 1)
                if g == PLAIN:
                    if some(i - 1):
                        act.wait_ge(low_p, i - 1)
                    nc.scalar.copy(p_t[e % 2][:, :], pt_ps[g % 2][:, :]).then_inc(plain, 1)

            def sums_out(i, e, g):
                if not real(i):
                    return
                m = g // 2
                act.wait_ge(pv_done, NG * i + g + 1)
                for j in range(2):
                    r = slice(64 * j, 64 * j + 64)
                    src = o_ps[m][r, 0:288].rearrange("p (n v) -> p n v", v=36)[:, :, 18 * j:18 * j + 18]
                    dst = os_all[r, bass.ds(i, 1), :].rearrange("p i (b n v) -> p (i n) b v", b=2, v=9)
                    nc.scalar.copy(dst[:, 8 * m:8 * m + 8, :, :],
                                   src.rearrange("p n (b v) -> p n b v", b=2)).then_inc(o_out, 1)

            def weights_high(cols):
                nc.scalar.copy(ew_hi[:, cols], ew[:, cols]).then_inc(ew_hi_ok, 1)

            def heads_out(c):
                act.wait_ge(otr_done, c + 1)
                if some(c):
                    act.wait_ge(wo_done, c)
                nc.scalar.copy(o_t[:, :], t_ps[:, :]).then_inc(ot_out, 1)

            def norm_out(c, r):
                act.wait_ge(ftr_done, c + 1)
                if some(c - 1):
                    act.wait_ge(h_done, FT * (c - 1))
                nc.scalar.copy(fn_hi[r][:, :], t_ps[:, :]).then_inc(fnh_out, 1)

            def logits_out(c):
                act.wait_ge(lg_done, c + 1)
                if some(c):
                    act.wait_ge(parts_done, c)
                src = t_ps[:, 0:TC * E]
                nc.scalar.activation(sig[:, :, :].rearrange("p i e -> p (i e)"), src, ACT.Exp, scale=-1.0).then_inc(lg_out, 1)
                nc.scalar.copy(logit[:, :, :].rearrange("p i e -> p (i e)"), src).then_inc(lg_out, 1)

            def gates_out(c, r):
                act.wait_ge(gtr_done, c + 1)
                if some(c - 1):
                    act.wait_ge(g_done, FT * (c - 1))
                nc.scalar.copy(gate_t[r][:, :], t_ps[:, :].bitcast(BF16)[0:96, 0:CW]).then_inc(gt_out, 1)

            def relu(c, f):
                n = FT * c + f
                act.wait_ge(h_done, n + 1)
                if some(n - 3):
                    act.wait_ge(gated, n - 3)
                nc.scalar.activation(hid[f % 4][:, :], h_ps[f % 2][:, :], ACT.Relu).then_inc(relu_done, 1)

            def high_hidden(c, f):
                n = FT * c + f
                act.wait_ge(gated, n + 1)
                if some(n - 7):
                    act.wait_ge(used, n - 7)
                    act.wait_ge(gh_low, n - 7)
                nc.scalar.copy(gh_hi[f % 8][:, :], ghid[f % 4][:, :]).then_inc(gh_high, 1)

            def y_copy(c, r):
                act.wait_ge(used, FT * c + FT)
                nc.scalar.copy(y_t[:, :], y_ps[r][:, :]).then_inc(y_out, 1)

            def store(c):
                act.wait_ge(y_sum, c + 1)
                act.dma_start(out_v[:, bass.ts(c, TC), :], x_all[:, bass.ts(c, TC), :]).then_inc(stored, 16)

            def chunk(c, r):
                for f in range(FT):
                    relu(c, f)
                    if f >= 1:
                        high_hidden(c, f - 1)
                    elif has(c, -1):
                        high_hidden(c - 1, FT - 1)
                    if f == 4 and has(c, -1):
                        y_copy(c - 1, 1 - r)
                    if f == 9 and has(c, -1):
                        store(c - 1)
                    if f == 9 and has(c, 1):
                        norm_out(c + 1, 1 - r)
                    if f == 11 and has(c, 1):
                        logits_out(c + 1)
                    if f == 13 and has(c, 2):
                        heads_out(c + 2)
                    if f == 15 and has(c, 1):
                        gates_out(c + 1, 1 - r)

            def head_start(k):
                if k == 4:
                    act.wait_ge(wp_in, N_WP)
                    nc.scalar.mul(rms_scaled[:, :], rms_col[:, :], 1.0 - LAMBDA_INIT).then_inc(rms_ok, 1)
                if k == 5:
                    act.wait_ge(rms_ok, 1)
                    nc.scalar.activation(wo[:, :, :], wo_raw[:, :, :], ACT.Copy, scale=rms_scaled[:, 0:1]).then_inc(wo_ok, 1)
                if k == 14:
                    heads_out(0)
                if k == 18:
                    norm_out(0, 0)
                if k == 20:
                    logits_out(0)
                if k == 22:
                    heads_out(1)
                if k == 25:
                    gates_out(0, 0)

            def tile_steps(i, e, last=False):
                for g in range(NG):
                    if g == 2:
                        pre_turn_out(*tile(i, e, 2))
                    exponent(*unit(i, e, g, EXP_LAG))
                    high_part(*unit(i, e, g, SPLIT_LAG))
                    if g == 0:
                        qk_high(*tile(i, e, 1))
                    if g in (1, 2):
                        one_head(*tile(i, e, 1), 2 * g - 2)
                        one_head(*tile(i, e, 1), 2 * g - 1)
                    if g == 3:
                        v_high(*tile(i, e, 2))
                    if g % 2 == 1:
                        sums_out(*unit(i, e, g, OUT_LAG))
                    if last:
                        head_start(i * NG + g - (NT - TB) * NG)

            act.wait_ge(heads_ok, 1)
            pre_turn_out(0, 0)
            v_high(0, 0)
            qk_high(0, 0)
            for j in range(NG):
                one_head(0, 0, j)
            pre_turn_out(1, 1)
            v_high(1, 1)
            act.wait_ge(sel_turned, 1)
            nc.scalar.copy(sel_hi[:, :], o_ps[0][:, 0:E]).then_inc(sel_hi_ok, 1)
            for e in range(TB):
                tile_steps(e, e)
                if e == 2:
                    act.wait_ge(lam_sums, 1)
                    nc.scalar.activation(lam_exp[:, :, :], lam_sum[:, :, :], ACT.Exp).then_inc(lam_exps, 1)
            act.wait_ge(ew_in, N_EW)
            with act.Fori(1, NB - 1) as t:
                for e in range(TB):
                    tile_steps(TB * t + e, e)
                    if e == 0:
                        weights_high(bass.ts(t - 1, PIECE))
            weights_high(slice(PIECE * (NB - 2), KW + VW))
            for e in range(TB + 3):
                tile_steps(NT - TB + e, e % TB, True)
            act.wait_ge(pv_done, NU)
            chunk(0, 0)
            with act.Fori(0, NC // 2 - 2) as u:
                chunk(2 * u + 1, 1)
                chunk(2 * u + 2, 0)
            for c in range(NC - 3, NC):
                chunk(c, c % 2)
            high_hidden(NC - 1, FT - 1)
            y_copy(NC - 1, 1)
            store(NC - 1)
            act.wait_ge(stored, 16 * NC)

        @block.vector
        def _(dve):
            own = [0]

            class Own:
                def add(self, ins):
                    own[0] += 1
                    ins.then_inc(dve_own, 1)

                def wait(self):
                    dve.wait_ge(dve_own, own[0])

                def __call__(self, ins):
                    self.add(ins)
                    self.wait()

            class Chain(Own):
                SEQ = 37

                def __init__(self, c):
                    self.base, self.n = c * self.SEQ, 0

                def add(self, ins):
                    self.n += 1
                    ins.then_inc(dve_seq, 1)

                def wait(self):
                    dve.wait_ge(dve_seq, self.base + self.n)

            one = Own()

            dve.wait_ge(ident_ok, 1)
            nc.vector.tensor_reduce(head_cols[:, :], ident[:, :].rearrange("p (g j d) -> p j g d", g=NG, j=NG),
                                    AX.XY, ALU.add).then_inc(heads_ok, 1)
            nc.vector.tensor_copy(ident_h[:, :], ident[:, :]).then_inc(consts_ok, 1)

            def root_estimate(ch, v, y):
                ch(nc.vector.tensor_scalar(y.bitcast(I32), v.bitcast(I32), -0.5, RSQRT_MAGIC, ALU.mult, ALU.add))

            def newton(ch, v, y, w, done=None):
                ch(nc.vector.tensor_tensor(w, y, y, ALU.mult))
                ch(nc.vector.scalar_tensor_tensor(out=w, in0=w, scalar=-0.5, in1=v, op0=ALU.mult, op1=ALU.mult))
                ins = nc.vector.scalar_tensor_tensor(out=y, in0=w, scalar=1.5, in1=y, op0=ALU.add, op1=ALU.mult)
                if done:
                    ins.then_inc(done, 1)
                else:
                    ch(ins)

            def moments(ch, st, mn, vr, tm):
                ch.add(nc.vector.tensor_tensor(tm, st[:, :, 1], st[:, :, 4], ALU.subtract))
                ch.add(nc.vector.tensor_tensor(mn, st[:, :, 1], st[:, :, 4], ALU.add))
                ch.add(nc.vector.tensor_tensor(vr, st[:, :, 2], st[:, :, 5], ALU.add))
                ch.wait()
                ch.add(nc.vector.tensor_tensor(tm, tm, tm, ALU.mult))
                ch.add(nc.vector.tensor_scalar(mn, mn, 0.5, None, ALU.mult))
                ch.wait()
                ch(nc.vector.scalar_tensor_tensor(out=vr, in0=tm, scalar=float(D) / 4, in1=vr,
                                                  op0=ALU.mult, op1=ALU.add))

            def x_roots(a, b):
                return var[:, a:b], rstd[:, a:b], tmp[:, a:b]

            def x_moments(a, b):
                moments(one, stats[:, a:b, :], mean[:, a:b], var[:, a:b], tmp[:, a:b])
                one(nc.vector.tensor_scalar(var[:, a:b], var[:, a:b], 1.0 / D, EPS, ALU.mult, ALU.add))
                root_estimate(one, *x_roots(a, b)[0:2])

            def norm_x(i, e):
                if not real(i):
                    return
                if some(i - 1):
                    dve.wait_ge(tr_done, i - 1)
                nc.vector.tensor_scalar(xn[e % 2][:, :], x_all[:, i, :], mean[:, bass.ds(i, 1)], rstd[:, bass.ds(i, 1)],
                                        ALU.subtract, ALU.mult).then_inc(xn_ready, 1)

            dve.wait_ge(x_in[0], 16)
            def x_stats(a, b):
                for i in range(a, b):
                    nc.vector.bn_stats(stats[:, i, :], x_all[:, i, :]).then_inc(dve_own, 1)
                own[0] += b - a

            x_stats(0, X0)
            dve.wait_ge(dve_own, own[0])
            x_moments(0, X0)
            for _ in range(3):
                newton(one, *x_roots(0, X0))
            norm_x(0, 0)
            norm_x(1, 1)
            nc.vector.tensor_copy(ident_bf[:, :], ident[:, :]).then_inc(consts_ok, 1)

            def qk_low(i, e, part):
                if not real(i):
                    return
                dve.wait_ge(qk_hi, 2 * i + 2)
                if some(i - 1):
                    dve.wait_ge(qm_lo_ok, 2 * (i - 1))
                    dve.wait_ge(scored, NG * (i - 1))
                if part == 0:
                    nc.vector.scalar_tensor_tensor(out=q_lo[e % 2][:, :], in0=m2_ps[:, 0:2 * P], scalar=QK_SCALE,
                                                   in1=q_hi[e % 2][:, :], op0=ALU.mult, op1=ALU.subtract).then_inc(qk_lo, 1)
                else:
                    nc.vector.tensor_tensor(k_lo[e % 2][:, :, :].rearrange("p h t -> p (h t)"), m2_ps[:, 2 * P:4 * P],
                                            k_hi[e % 2][:, :, :].rearrange("p h t -> p (h t)"), ALU.subtract).then_inc(qk_lo, 1)

            def v_low(i, e):
                if not real(i):
                    return
                dve.wait_ge(v_hi_out, 2 * i + 2)
                if some(i - 3):
                    dve.wait_ge(pv_done, NG * (i - 3))
                for b in range(2):
                    r = slice(64 * b, 64 * b + 64)
                    nc.vector.tensor_tensor(v_lo[e][r, :, :, b, 0:8].rearrange("p n j v -> p (n j) v"),
                                            m_ps[r, 2 * P:3 * P].rearrange("p (n v) -> p n v", v=DH),
                                            v_hi[e][r, :, :, b, 0:8].rearrange("p n j v -> p (n j) v"),
                                            ALU.subtract).then_inc(v_lo_out, 1)

            def add_mask(i, e, g, nth):
                if not real(i):
                    return
                n = NG * i + g
                dve.wait_ge(scored, n + 1)
                if g == 0:
                    dve.wait_ge(mask_in[e % 2], 32 * nth)
                if some(n - 7):
                    dve.wait_ge(turned, n - 7)
                m = mask_sb[e % 2][:, g, :, :, :].rearrange("p r b k -> p r (b k)").unsqueeze(2).to_broadcast([P, 2, 2, P])
                nc.vector.tensor_tensor(prob[4 * (e % 2) + g][:, :, :, :].rearrange("p (r h) b k -> p r h (b k)", r=2),
                                        sc_ps[g % 2][:, :].rearrange("p (r h k) -> p r h k", r=2, h=2),
                                        m, ALU.add).then_inc(masked, 1)

            def row_max(i, e, g):
                if not real(i):
                    return
                n = NG * i + g
                dve.wait_ge(masked, n + 1)
                if some(n - 3):
                    dve.wait_ge(shifted, n - 3)
                nc.vector.tensor_reduce(rowmax[g][:, :], prob[4 * (e % 2) + g][:, :, :, :].rearrange("p a b k -> p (a b) k"),
                                        AX.X, ALU.max).then_inc(maxed, 1)

            def low_part(i, e, g):
                if not real(i) or g == PLAIN:
                    return
                dve.wait_ge(high, NG * i + g + 1)
                nc.vector.tensor_tensor(p_lo[g][:, :, :].rearrange("p a k -> p (a k)"), pt_ps[g % 2][:, :],
                                        p_hi[g][:, :, :].rearrange("p a k -> p (a k)"),
                                        ALU.subtract).then_inc(low_v, 1)

            def lambda_sums():
                dve.wait_ge(lam_in_s, N_LAM)
                for a in range(2):
                    one(nc.vector.tensor_tensor(lam_prod[:, a, :], lam_in[:, 2 * a, :], lam_in[:, 2 * a + 1, :], ALU.mult))
                nc.vector.tensor_reduce(lam_sum[:, :, :].rearrange("p a h -> p (a h)"),
                                        lam_prod[:, :, :].rearrange("p a (h d) -> p (a h) d", d=DH),
                                        AX.X, ALU.add).then_inc(lam_sums, 1)

            def lambdas():
                dve.wait_ge(lam_exps, 1)
                one(nc.vector.tensor_tensor(lam_all[:, :], lam_exp[:, 0, :], lam_exp[:, 1, :], ALU.subtract))
                one(nc.vector.tensor_scalar(lam_all[:, :], lam_all[:, :], LAMBDA_INIT, None, ALU.add))
                for j in range(2):
                    r = slice(64 * j, 64 * j + 64)
                    for b in range(2):
                        one(nc.vector.tensor_copy(lam[r, b, :], lam_all[r, :].rearrange("p (n j) -> p n j", j=2)[:, :, j]))

            def selectors_low():
                dve.wait_ge(sel_hi_ok, 1)
                nc.vector.tensor_tensor(sel_lo[:, :], o_ps[0][:, 0:E], sel_hi[:, :], ALU.subtract).then_inc(sel_lo_ok, 1)

            def inverse_sums(c):
                if some(c):
                    dve.wait_ge(sq_done, c)
                os_c = os_all[:, bass.ts(c, TC), :].rearrange("p i (n v) -> p (i n) v", v=9)
                nc.vector.reciprocal(linv[:, :, :].rearrange("p n h -> p (n h)").unsqueeze(2),
                                     os_c[:, :, 8:9]).then_inc(inv_own, 1)
                dve.wait_ge(inv_own, c + 1)
                lv = linv[:, :, 1].rearrange("p (i n) -> p i n", i=TC)
                lm = lam[:, :, :].rearrange("p b n -> p (b n)").unsqueeze(1).to_broadcast([P, TC, 2 * HP])
                nc.vector.tensor_tensor(lv, lv, lm, ALU.mult).then_inc(inv_done, 1)

            def mean_squares(c, ch):
                dve.wait_ge(sq_done, c + 1)
                if some(c):
                    dve.wait_ge(on_done, c)
                ch(nc.vector.tensor_reduce(sq_v[:, 0:64], osq[:, :, :], AX.X, ALU.add))
                ch.add(nc.vector.tensor_scalar(sq_v[:, 0:64], sq_v[:, 0:64], 1.0 / DH, EPS, ALU.mult, ALU.add))

            def residual(c, ps=w_ps):
                dve.wait_ge(wo_done, c + 1)
                for b in range(2):
                    r = slice(64 * b, 64 * b + 64)
                    xr = x_all[r, bass.ts(c, TC), :].rearrange("p i d -> p (i d)")
                    nc.vector.tensor_tensor(xr, xr, ps[r, :], ALU.add).then_inc(res_done, 1)

            def token_stats(c, ch):
                dve.wait_ge(res_done, 2 * (c + 1))
                dve.nop(nofuse=True)
                for ii in range(TC):
                    ch.add(nc.vector.bn_stats(fstats[:, ii, :], x_all[:, bass.ds(c * TC + ii, 1), :].rearrange("p i d -> p (i d)")))
                ch.wait()

            def variances(c, ch):
                ch(nc.vector.tensor_scalar(sq_v[:, 64:64 + TC], fvar[:, :], 1.0 / D, EPS, ALU.mult, ALU.add))

            def normalise(c):
                dve.wait_ge(rr_done, c + 2)
                if some(c):
                    dve.wait_ge(ftr_done, c)
                for ii in range(TC):
                    nc.vector.tensor_scalar(fn[:, ii, :], x_all[:, bass.ds(c * TC + ii, 1), :].rearrange("p i d -> p (i d)"),
                                            fmean[:, ii:ii + 1], sq_y[:, 64 + ii:65 + ii],
                                            ALU.subtract, ALU.mult).then_inc(fn_done, 1)

            def norm_low(c, r):
                dve.wait_ge(fnh_out, c + 1)
                if some(c - 1):
                    dve.wait_ge(h_done, FT * (c - 1))
                nc.vector.tensor_tensor(fn_lo[r][:, :], t_ps[:, :], fn_hi[r][:, :], ALU.subtract).then_inc(fnl_out, 1)

            def sigmoid(c, ch):
                dve.wait_ge(lg_out, 2 * c + 2)
                ch(nc.vector.tensor_scalar(sig[:, :, :], sig[:, :, :], 1.0, None, ALU.add))
                ch.add(nc.vector.reciprocal(sig[:, :, :], sig[:, :, :]))

            def choose(c, ch):
                for ii in range(TC):
                    ch.add(nc.vector.max(top8[:, ii, :], logit[:, ii, :]))
                ch.wait()
                ch(nc.vector.memset(top8[:, :, TOPK:8], NOMATCH))
                dve.nop(nofuse=True)
                for ii in range(TC):
                    ch.add(nc.vector.match_replace(rest[:, ii, :], top8[:, ii, :], logit[:, ii, :], HIDE))
                ch.wait()

            def gate_parts(c, ch):
                ch(nc.vector.scalar_tensor_tensor(out=gate[:, :, :].rearrange("p i e -> p (i e)"),
                                                  in0=rest[:, :, :].rearrange("p i e -> p (i e)"), scalar=HIDE,
                                                  in1=sig[:, :, :].rearrange("p i e -> p (i e)"),
                                                  op0=ALU.is_equal, op1=ALU.mult))
                if some(c):
                    dve.wait_ge(gtr_done, c)
                ch(nc.vector.tensor_copy(gpart[:, :, 0, :], gate[:, :, :]))
                ch(nc.vector.tensor_tensor(gate[:, :, :], gate[:, :, :], gpart[:, :, 0, :], ALU.subtract))
                ch(nc.vector.tensor_copy(gpart[:, :, 1, :], gate[:, :, :]))
                nc.vector.tensor_tensor(gpart[:, :, 2, :], gate[:, :, :], gpart[:, :, 1, :], ALU.subtract).then_inc(parts_done, 1)

            def apply_gate(c, f):
                n = FT * c + f
                dve.wait_ge(relu_done, n + 1)
                dve.wait_ge(g_done, n + 1)
                if some(n - 3):
                    dve.wait_ge(gh_low, n - 3)
                nc.vector.tensor_tensor(ghid[f % 4][:, :], g_ps[f % 2][:, :], hid[f % 4][:, :], ALU.mult).then_inc(gated, 1)

            def final_add(c):
                dve.wait_ge(y_turned, c + 1)
                xc = x_all[:, bass.ts(c, TC), :].rearrange("p i d -> p (i d)")
                nc.vector.tensor_tensor(xc, xc, w_ps[:, :], ALU.add).then_inc(y_sum, 1)

            def chunk(c, r):
                ch = Chain(c)
                cols = slice(0, 64 + TC) if has(c, 2) else slice(64, 64 + TC)
                roots = sq_v[:, cols], sq_y[:, cols], sq_w[:, cols]
                for f in range(FT):
                    apply_gate(c, f)
                    if f == 0 and has(c, 1):
                        token_stats(c + 1, ch)
                    if f == 1 and has(c, 2):
                        mean_squares(c + 2, ch)
                    if f == 2 and has(c, 1):
                        moments(ch, fstats, fmean[:, :], fvar[:, :], ftmp[:, :])
                    if f == 3 and has(c, 1):
                        variances(c + 1, ch)
                        root_estimate(ch, *roots[0:2])
                    if f in (3, 4) and has(c, 1):
                        newton(ch, *roots)
                    if f == 5 and has(c, 1):
                        newton(ch, *roots, rr_done)
                    if f == 6 and has(c, 1):
                        normalise(c + 1)
                    if f == 7 and has(c, -1):
                        final_add(c - 1)
                    if f == 9 and has(c, 1):
                        norm_low(c + 1, 1 - r)
                    if f == 10 and has(c, 3):
                        inverse_sums(c + 3)
                    if f == 11 and has(c, 1):
                        sigmoid(c + 1, ch)
                    if f == 12 and has(c, 1):
                        choose(c + 1, ch)
                    if f == 13 and has(c, 1):
                        gate_parts(c + 1, ch)
                    if f == 14 and has(c, 2):
                        residual(c + 2)
                assert not has(c, 2) or ch.n == Chain.SEQ, ch.n

            def first_start(k):
                if k == 0:
                    dve.wait_ge(x_in[1], 16)
                if k < 4:
                    x_stats(X0 + k * (NT - X0) // 4, X0 + (k + 1) * (NT - X0) // 4)
                if k == 4:
                    dve.wait_ge(dve_own, own[0])
                    x_moments(X0, NT)
                if 5 <= k < 8:
                    newton(one, *x_roots(X0, NT))
                if k == 10:
                    lambda_sums()
                if k == 14:
                    lambdas()

            head_roots = sq_v[:, 0:64], sq_y[:, 0:64], sq_w[:, 0:64]
            roots = sq_v[:, :], sq_y[:, :], sq_w[:, :]

            def head_start(k):
                if k == 3:
                    inverse_sums(0)
                if k == 8:
                    mean_squares(0, one)
                if k == 9:
                    one.wait()
                    root_estimate(one, *head_roots[0:2])
                    newton(one, *head_roots)
                if k == 10:
                    newton(one, *head_roots)
                if k == 11:
                    newton(one, *head_roots, rr_done)
                if k == 12:
                    inverse_sums(1)
                if k == 15:
                    residual(0, m_ps)
                if k == 16:
                    token_stats(0, one)
                    moments(one, fstats, fmean[:, :], fvar[:, :], ftmp[:, :])
                    mean_squares(1, one)
                    variances(0, one)
                    root_estimate(one, *roots[0:2])
                if k == 17:
                    newton(one, *roots)
                    newton(one, *roots)
                    newton(one, *roots, rr_done)
                    normalise(0)
                if k == 19:
                    norm_low(0, 0)
                if k == 21:
                    sigmoid(0, one)
                if k == 22:
                    choose(0, one)
                if k == 23:
                    gate_parts(0, one)
                if k == 24:
                    inverse_sums(2)
                    residual(1)

            def tile_steps(i, e, nth, beside=None):
                for g in range(NG):
                    if g == 0:
                        norm_x(*tile(i, e, 2))
                        v_low(*tile(i, e, 1))
                    if g in (1, 2):
                        qk_low(*tile(i, e, 1), g - 1)
                    add_mask(i, e, g, nth)
                    row_max(*unit(i, e, g, 1))
                    low_part(*unit(i, e, g, SPLIT_LAG))
                    if beside:
                        beside((i * NG + g) if i < TB else i * NG + g - (NT - TB) * NG)

            v_low(0, 0)
            qk_low(0, 0, 0)
            qk_low(0, 0, 1)
            selectors_low()
            for e in range(TB):
                tile_steps(e, e, e // 2 + 1, first_start)
            with dve.Fori(1, NB - 1) as t:
                for e in range(TB):
                    tile_steps(TB * t + e, e, 2 * t + e // 2 + 1)
            for e in range(TB + 3):
                tile_steps(NT - TB + e, e % TB, 2 * (NB - 1) + e // 2 + 1, head_start)
            dve.wait_ge(turned, NU)
            chunk(0, 0)
            with dve.Fori(0, NC // 2 - 2) as u:
                chunk(2 * u + 1, 1)
                chunk(2 * u + 2, 0)
            for c in range(NC - 3, NC):
                chunk(c, c % 2)
            final_add(NC - 1)


_INS = ['x', 'ctx_1024', 'mask_Bx16xSxS2_ff0', 'L0_xattn_W_q', 'L0_xattn_W_k', 'L0_xattn_W_v', 'L0_xattn_W_o',
        'L0_xattn_lambda_q1', 'L0_xattn_lambda_k1', 'L0_xattn_lambda_q2', 'L0_xattn_lambda_k2',
        'L0_xattn_rms_scale', 'L0_ffn_expert_sel', 'L0_ffn_keys', 'L0_ffn_values']
_OUTS = [((B, S, D), 'float32')]


def kernel(**inputs):
    import numpy as _np
    import concourse.bacc as _bacc
    from concourse import mybir as _mybir
    from concourse.bass_utils import run_bass_kernel_spmd as _run

    nc = _bacc.Bacc("TRN2", target_bir_lowering=False, num_devices=1)
    arrays, args = {}, []
    for name in _INS:
        a = _np.ascontiguousarray(inputs[name])
        arrays[f"in_{name}_dram"] = a
        args.append(nc.dram_tensor(f"in_{name}_dram", a.shape, _mybir.dt.from_np(a.dtype), kind="ExternalInput").ap())
    for i, (shape, dtype) in enumerate(_OUTS):
        dt = _mybir.dt.from_np(_np.dtype(dtype))
        args.append(nc.dram_tensor(f"out_{i}_dram", shape, dt, kind="ExternalOutput").ap())
    xattn_ffn(nc, *args)
    r = _run(nc, [arrays], core_ids=[0])
    return r.results[0]["out_0_dram"]
```
